# Optimizing a Trainium2 kernel written in Bass

```python
import numpy as np
import jax
import jax.numpy as jnp

def _softmax(x, axis=-1):
    return jax.nn.softmax(x, axis=axis)

def _gelu(x):
    return jax.nn.gelu(x, approximate=True)

def _silu(x):
    return jax.nn.silu(x)

def _sigmoid(x):
    return jax.nn.sigmoid(x)

def _layernorm(x, axis=-1, eps=1e-05):
    m = jnp.mean(x, axis=axis, keepdims=True)
    v = jnp.var(x, axis=axis, keepdims=True)
    return (x - m) / jnp.sqrt(v + eps)

def _scatter_add(tgt, idx, src, axis=0):
    return tgt.at[idx].add(src)

def _segment_sum(src, seg, n):
    return jax.ops.segment_sum(src, seg, n)
kernel_name = 'mk_conv_preact_d4_conv_nchw512_r2_92a75c'

def setup_inputs(seed: int=0):
    np.random.seed(seed)
    _w = jnp.asarray

    def _rec_inputs():
        import jax
        import jax.numpy as jnp
        _gk = jax.random.key(seed)
        x = 0.4999 + 0.2886 * jax.random.normal(jax.random.fold_in(_gk, 1), (32, 256, 28, 28), jnp.float32)
        return x
    x = _rec_inputs()

    def _L0_conv_setup():
        import jax, jax.numpy as jnp
        import numpy as np
        from jax import lax

        def _get_mu(x):
            bs, depth, h, w = x.shape
            ix = jnp.arange(1, h + 1, dtype=x.dtype).reshape(1, 1, h, 1)
            iy = jnp.arange(1, w + 1, dtype=x.dtype).reshape(1, 1, 1, w)
            sumX = jnp.maximum(x.sum((2, 3)), 1e-09)
            mu_x = jnp.maximum(jnp.round((ix * x).sum((2, 3)) / sumX), 1.0)
            mu_y = jnp.maximum(jnp.round((iy * x).sum((2, 3)) / sumX), 1.0)
            lin = jnp.linspace(-1.0, 1.0, h, dtype=x.dtype)
            mu_xg = lin[(mu_x - 1.0).astype(jnp.int32)]
            mu_yg = lin[(mu_y - 1.0).astype(jnp.int32)]
            return (mu_xg, mu_yg)

        def _get_mask(x, mask_weight, filt):
            bs, depth, h, w = x.shape
            mu_x, mu_y = _get_mu(x)
            posX = jnp.linspace(-1.0, 1.0, h, dtype=x.dtype).reshape(1, 1, h, 1)
            posY = jnp.linspace(-1.0, 1.0, w, dtype=x.dtype).reshape(1, 1, 1, w)
            m = jnp.abs(posX - mu_x[:, :, None, None]) + jnp.abs(posY - mu_y[:, :, None, None])
            m = 1.0 - m * mask_weight.reshape(1, depth, 1, 1)
            m = jnp.maximum(m, -1.0)
            m = jnp.where(filt.reshape(1, depth, 1, 1) == 1.0, m, 1.0)
            return m
        key = jax.random.key(seed)
        k1, k2, k3, k4 = jax.random.split(key, 4)
        bs, depth, h, w = (32, 256, 28, 28)
        out_c, kh, kw = (256, 3, 3)
        x = jax.random.uniform(k1, (bs, depth, h, w), dtype=jnp.float32)
        weight = jax.random.normal(k2, (out_c, depth, kh, kw), dtype=jnp.float32) * 0.02
        bias = jax.random.normal(k3, (out_c,), dtype=jnp.float32) * 0.02
        mask_weight = jax.random.uniform(k4, (depth,), dtype=jnp.float32)
        filt = jnp.ones((depth, 1), dtype=jnp.float32)
        return {'x': x, 'weight': weight, 'bias': bias, 'mask_weight': mask_weight, 'filter': filt, 'padding': 1}
    _L0_conv_all = _L0_conv_setup()
    _L0_conv_in = {k: v for k, v in _L0_conv_all.items() if k in ('weight', 'bias', 'mask_weight', 'filter')}
    del _L0_conv_all

    def _L1_conv_setup():
        import jax, jax.numpy as jnp
        from jax import lax
        import numpy as np
        UP = 2
        DOWN = 2
        PADDING = (11, 10, 11, 10)
        GAIN = float(np.sqrt(2.0))
        SLOPE = 0.2
        CLAMP = 256.0
        UP_TAPS = 12
        IN_CUTOFF = 8.0
        OUT_CUTOFF = 8.0
        IN_HALF_WIDTH = 6.0
        OUT_HALF_WIDTH = 6.0
        TEMP_FS = 32.0

        def _design_lowpass(numtaps, cutoff, width, fs):
            nyq = fs / 2.0
            atten = 2.285 * (numtaps - 1) * np.pi * (width / nyq) + 7.95
            if atten > 50.0:
                beta = 0.1102 * (atten - 8.7)
            elif atten > 21.0:
                beta = 0.5842 * (atten - 21.0) ** 0.4 + 0.07886 * (atten - 21.0)
            else:
                beta = 0.0
            m = np.arange(numtaps) - (numtaps - 1) / 2.0
            c = cutoff / nyq
            h = c * np.sinc(c * m)
            h = h * np.kaiser(numtaps, beta)
            h = h / np.sum(h)
            return h.astype(np.float32)

        def _upfirdn2d_sep(x, f, up, down, pad, gain):
            N, C, H, W = x.shape
            fr = f[::-1].astype(x.dtype)
            kH = fr.reshape(1, 1, -1, 1)
            kW = fr.reshape(1, 1, 1, -1)
            px0, px1, py0, py1 = pad
            xr = x.reshape(N * C, 1, H, W)
            xr = lax.conv_general_dilated(xr, kH, window_strides=(down, 1), padding=((py0, py1 + up - 1), (0, 0)), lhs_dilation=(up, 1))
            xr = lax.conv_general_dilated(xr, kW, window_strides=(1, down), padding=((0, 0), (px0, px1 + up - 1)), lhs_dilation=(1, up))
            Ho, Wo = (xr.shape[2], xr.shape[3])
            return xr.reshape(N, C, Ho, Wo) * gain
        key = jax.random.key(seed)
        k1, k2 = jax.random.split(key)
        x = jax.random.normal(k1, (8, 256, 32, 32), dtype=jnp.float32)
        bias = jax.random.normal(k2, (256,), dtype=jnp.float32) * 0.1
        up_filter = jnp.asarray(_design_lowpass(UP_TAPS, IN_CUTOFF, IN_HALF_WIDTH * 2, TEMP_FS))
        down_filter = jnp.asarray(_design_lowpass(UP_TAPS, OUT_CUTOFF, OUT_HALF_WIDTH * 2, TEMP_FS))
        return {'x': x, 'bias': bias, 'up_filter': up_filter, 'down_filter': down_filter}
    _L1_conv_all = _L1_conv_setup()
    _L1_conv_in = {k: v for k, v in _L1_conv_all.items() if k in ('bias', 'up_filter', 'down_filter')}
    del _L1_conv_all

    def _L2_conv_setup():
        import jax, jax.numpy as jnp
        from jax import lax
        import numpy as np
        D_IN = 256
        HID = 64
        D_INNER = 2 * HID
        D_PROJ = 2 * D_INNER
        N_STATE = 16
        R_DT = 8
        B, H, W = (8, 32, 32)

        def _layernorm(y, g, b):
            mu = y.mean(-1, keepdims=True)
            var = ((y - mu) ** 2).mean(-1, keepdims=True)
            return (y - mu) / jnp.sqrt(var + 1e-05) * g + b

        def _ssm(x, xw, dtw, dtb, Al, Dv, g, be):
            Bb, D, L = x.shape
            n = Al.shape[1]
            xd = jnp.einsum('bdl,kd->blk', x, xw)
            dts = xd[..., :R_DT]
            Bs = xd[..., R_DT:R_DT + n]
            Cs = xd[..., R_DT + n:]
            delta = jax.nn.softplus(jnp.einsum('blr,dr->bld', dts, dtw) + dtb)
            A = -jnp.exp(Al)
            xt = x.transpose(0, 2, 1)
            dA = jnp.exp(delta[..., None] * A)
            dBx = delta[..., None] * Bs[:, :, None, :] * xt[..., None]

            def step(h, inp):
                da, dbx, c = inp
                h = h * da + dbx
                return (h, jnp.einsum('bdn,bn->bd', h, c))
            h0 = jnp.zeros((Bb, D, n), x.dtype)
            _, ys = lax.scan(step, h0, (dA.transpose(1, 0, 2, 3), dBx.transpose(1, 0, 2, 3), Cs.transpose(1, 0, 2)))
            y = ys.transpose(1, 0, 2) + xt * Dv
            return _layernorm(y, g, be)

        def _up2(y, h, w):
            Bb, L, C = y.shape
            img = y.transpose(0, 2, 1).reshape(Bb, C, h, w)
            img = jnp.repeat(jnp.repeat(img, 2, axis=2), 2, axis=3)
            return img.reshape(Bb, C, 4 * L).transpose(0, 2, 1)

        def _conv1x1(x, w, b):
            return jnp.einsum('bchw,oc->bohw', x, w) + b[None, :, None, None]

        def _conv2s2(x, w, b):
            out = lax.conv_general_dilated(x, w, (2, 2), 'VALID', dimension_numbers=('NCHW', 'OIHW', 'NCHW'))
            return out + b[None, :, None, None]

        def _forward(input_f, in_w, in_b, c1_w, c1_b, c2_w, c2_b, c3_w, c3_b, out_w, out_b, xw1, dtw1, dtb1, Al1, Dv1, g1, be1, xw2, dtw2, dtb2, Al2, Dv2, g2, be2, xw3, dtw3, dtb3, Al3, Dv3, g3, be3):
            xz = _conv1x1(input_f, in_w, in_b)
            x, z = jnp.split(xz, 2, axis=1)
            f1 = _conv1x1(x, c1_w, c1_b)
            f2 = _conv2s2(f1, c2_w, c2_b)
            f3 = _conv2s2(f2, c3_w, c3_b)
            Bb, C, h3, w3 = f3.shape
            fx3 = f3.reshape(Bb, C, h3 * w3)
            y3 = _ssm(fx3, xw3, dtw3, dtb3, Al3, Dv3, g3, be3) + jnp.flip(_ssm(jnp.flip(fx3, -1), xw3, dtw3, dtb3, Al3, Dv3, g3, be3), 1)
            y2_ = _up2(y3, h3, w3)
            _, _, h2, w2 = f2.shape
            fx2 = f2.reshape(Bb, C, h2 * w2)
            y2 = _ssm(fx2, xw2, dtw2, dtb2, Al2, Dv2, g2, be2) + jnp.flip(_ssm(jnp.flip(fx2, -1), xw2, dtw2, dtb2, Al2, Dv2, g2, be2), 1) + y2_
            y1_ = _up2(y2, h2, w2)
            _, _, h1, w1 = f1.shape
            fx1 = f1.reshape(Bb, C, h1 * w1)
            y1 = _ssm(fx1, xw1, dtw1, dtb1, Al1, Dv1, g1, be1) + jnp.flip(_ssm(jnp.flip(fx1, -1), xw2, dtw2, dtb2, Al2, Dv2, g2, be2), 1) + y1_
            out1 = y1.transpose(0, 2, 1).reshape(Bb, C, h1, w1)
            out = out1 * jax.nn.silu(z)
            return _conv1x1(out, out_w, out_b)
        key = jax.random.key(seed)
        ks = iter(jax.random.split(key, 32))

        def nrm(shape, s=0.05):
            return jax.random.normal(next(ks), shape, dtype=jnp.float32) * s
        inp = {'input_f': jax.random.normal(next(ks), (B, D_IN, H, W), dtype=jnp.float32), 'in_w': nrm((D_PROJ, D_IN)), 'in_b': nrm((D_PROJ,)), 'c1_w': nrm((D_INNER, D_INNER)), 'c1_b': nrm((D_INNER,)), 'c2_w': nrm((D_INNER, D_INNER, 2, 2)), 'c2_b': nrm((D_INNER,)), 'c3_w': nrm((D_INNER, D_INNER, 2, 2)), 'c3_b': nrm((D_INNER,)), 'out_w': nrm((D_IN, D_INNER)), 'out_b': nrm((D_IN,))}
        Al = jnp.log(jnp.tile(jnp.arange(1, N_STATE + 1, dtype=jnp.float32), (D_INNER, 1)))
        for i in (1, 2, 3):
            inp[f'xw{i}'] = nrm((R_DT + 2 * N_STATE, D_INNER))
            inp[f'dtw{i}'] = nrm((D_INNER, R_DT), s=R_DT ** (-0.5))
            inp[f'dtb{i}'] = nrm((D_INNER,)) - 4.0
            inp[f'Al{i}'] = Al
            inp[f'Dv{i}'] = jnp.ones((D_INNER,), jnp.float32)
            inp[f'g{i}'] = jnp.ones((D_INNER,), jnp.float32)
            inp[f'be{i}'] = jnp.zeros((D_INNER,), jnp.float32)
        return inp
    _L2_conv_all = _L2_conv_setup()
    _L2_conv_in = {k: v for k, v in _L2_conv_all.items() if k in ('in_w', 'in_b', 'c1_w', 'c1_b', 'c2_w', 'c2_b', 'c3_w', 'c3_b', 'out_w', 'out_b', 'xw1', 'dtw1', 'dtb1', 'Al1', 'Dv1', 'g1', 'be1', 'xw2', 'dtw2', 'dtb2', 'Al2', 'Dv2', 'g2', 'be2', 'xw3', 'dtw3', 'dtb3', 'Al3', 'Dv3', 'g3', 'be3')}
    del _L2_conv_all

    def _L3_conv_setup():
        import jax, jax.numpy as jnp
        from jax import lax
        import numpy as np
        UP = 2
        DOWN = 2
        PADDING = (11, 10, 11, 10)
        GAIN = float(np.sqrt(2.0))
        SLOPE = 0.2
        CLAMP = 256.0
        UP_TAPS = 12
        IN_CUTOFF = 8.0
        OUT_CUTOFF = 8.0
        IN_HALF_WIDTH = 6.0
        OUT_HALF_WIDTH = 6.0
        TEMP_FS = 32.0

        def _design_lowpass(numtaps, cutoff, width, fs):
            nyq = fs / 2.0
            atten = 2.285 * (numtaps - 1) * np.pi * (width / nyq) + 7.95
            if atten > 50.0:
                beta = 0.1102 * (atten - 8.7)
            elif atten > 21.0:
                beta = 0.5842 * (atten - 21.0) ** 0.4 + 0.07886 * (atten - 21.0)
            else:
                beta = 0.0
            m = np.arange(numtaps) - (numtaps - 1) / 2.0
            c = cutoff / nyq
            h = c * np.sinc(c * m)
            h = h * np.kaiser(numtaps, beta)
            h = h / np.sum(h)
            return h.astype(np.float32)

        def _upfirdn2d_sep(x, f, up, down, pad, gain):
            N, C, H, W = x.shape
            fr = f[::-1].astype(x.dtype)
            kH = fr.reshape(1, 1, -1, 1)
            kW = fr.reshape(1, 1, 1, -1)
            px0, px1, py0, py1 = pad
            xr = x.reshape(N * C, 1, H, W)
            xr = lax.conv_general_dilated(xr, kH, window_strides=(down, 1), padding=((py0, py1 + up - 1), (0, 0)), lhs_dilation=(up, 1))
            xr = lax.conv_general_dilated(xr, kW, window_strides=(1, down), padding=((0, 0), (px0, px1 + up - 1)), lhs_dilation=(1, up))
            Ho, Wo = (xr.shape[2], xr.shape[3])
            return xr.reshape(N, C, Ho, Wo) * gain
        key = jax.random.key(seed)
        k1, k2 = jax.random.split(key)
        x = jax.random.normal(k1, (8, 256, 32, 32), dtype=jnp.float32)
        bias = jax.random.normal(k2, (256,), dtype=jnp.float32) * 0.1
        up_filter = jnp.asarray(_design_lowpass(UP_TAPS, IN_CUTOFF, IN_HALF_WIDTH * 2, TEMP_FS))
        down_filter = jnp.asarray(_design_lowpass(UP_TAPS, OUT_CUTOFF, OUT_HALF_WIDTH * 2, TEMP_FS))
        return {'x': x, 'bias': bias, 'up_filter': up_filter, 'down_filter': down_filter}
    _L3_conv_all = _L3_conv_setup()
    _L3_conv_in = {k: v for k, v in _L3_conv_all.items() if k in ('bias', 'up_filter', 'down_filter')}
    del _L3_conv_all
    return {'x': x, 'L0_conv_weight': _L0_conv_in['weight'], 'L0_conv_bias': _L0_conv_in['bias'], 'L0_conv_mask_weight': _L0_conv_in['mask_weight'], 'L0_conv_filter': _L0_conv_in['filter'], 'L1_conv_bias': _L1_conv_in['bias'], 'L1_conv_up_filter': _L1_conv_in['up_filter'], 'L1_conv_down_filter': _L1_conv_in['down_filter'], 'L2_conv_in_w': _L2_conv_in['in_w'], 'L2_conv_in_b': _L2_conv_in['in_b'], 'L2_conv_c1_w': _L2_conv_in['c1_w'], 'L2_conv_c1_b': _L2_conv_in['c1_b'], 'L2_conv_c2_w': _L2_conv_in['c2_w'], 'L2_conv_c2_b': _L2_conv_in['c2_b'], 'L2_conv_c3_w': _L2_conv_in['c3_w'], 'L2_conv_c3_b': _L2_conv_in['c3_b'], 'L2_conv_out_w': _L2_conv_in['out_w'], 'L2_conv_out_b': _L2_conv_in['out_b'], 'L2_conv_xw1': _L2_conv_in['xw1'], 'L2_conv_dtw1': _L2_conv_in['dtw1'], 'L2_conv_dtb1': _L2_conv_in['dtb1'], 'L2_conv_Al1': _L2_conv_in['Al1'], 'L2_conv_Dv1': _L2_conv_in['Dv1'], 'L2_conv_g1': _L2_conv_in['g1'], 'L2_conv_be1': _L2_conv_in['be1'], 'L2_conv_xw2': _L2_conv_in['xw2'], 'L2_conv_dtw2': _L2_conv_in['dtw2'], 'L2_conv_dtb2': _L2_conv_in['dtb2'], 'L2_conv_Al2': _L2_conv_in['Al2'], 'L2_conv_Dv2': _L2_conv_in['Dv2'], 'L2_conv_g2': _L2_conv_in['g2'], 'L2_conv_be2': _L2_conv_in['be2'], 'L2_conv_xw3': _L2_conv_in['xw3'], 'L2_conv_dtw3': _L2_conv_in['dtw3'], 'L2_conv_dtb3': _L2_conv_in['dtb3'], 'L2_conv_Al3': _L2_conv_in['Al3'], 'L2_conv_Dv3': _L2_conv_in['Dv3'], 'L2_conv_g3': _L2_conv_in['g3'], 'L2_conv_be3': _L2_conv_in['be3'], 'L3_conv_bias': _L3_conv_in['bias'], 'L3_conv_up_filter': _L3_conv_in['up_filter'], 'L3_conv_down_filter': _L3_conv_in['down_filter']}

def reference(x, L0_conv_weight, L0_conv_bias, L0_conv_mask_weight, L0_conv_filter, L1_conv_bias, L1_conv_up_filter, L1_conv_down_filter, L2_conv_in_w, L2_conv_in_b, L2_conv_c1_w, L2_conv_c1_b, L2_conv_c2_w, L2_conv_c2_b, L2_conv_c3_w, L2_conv_c3_b, L2_conv_out_w, L2_conv_out_b, L2_conv_xw1, L2_conv_dtw1, L2_conv_dtb1, L2_conv_Al1, L2_conv_Dv1, L2_conv_g1, L2_conv_be1, L2_conv_xw2, L2_conv_dtw2, L2_conv_dtb2, L2_conv_Al2, L2_conv_Dv2, L2_conv_g2, L2_conv_be2, L2_conv_xw3, L2_conv_dtw3, L2_conv_dtb3, L2_conv_Al3, L2_conv_Dv3, L2_conv_g3, L2_conv_be3, L3_conv_bias, L3_conv_up_filter, L3_conv_down_filter):
    import jax
    import jax.numpy as jnp

    def _L0_conv_ref(x, weight, bias, mask_weight, filter, padding):
        import jax, jax.numpy as jnp
        import numpy as np
        from jax import lax

        def _get_mu(x):
            bs, depth, h, w = x.shape
            ix = jnp.arange(1, h + 1, dtype=x.dtype).reshape(1, 1, h, 1)
            iy = jnp.arange(1, w + 1, dtype=x.dtype).reshape(1, 1, 1, w)
            sumX = jnp.maximum(x.sum((2, 3)), 1e-09)
            mu_x = jnp.maximum(jnp.round((ix * x).sum((2, 3)) / sumX), 1.0)
            mu_y = jnp.maximum(jnp.round((iy * x).sum((2, 3)) / sumX), 1.0)
            lin = jnp.linspace(-1.0, 1.0, h, dtype=x.dtype)
            mu_xg = lin[(mu_x - 1.0).astype(jnp.int32)]
            mu_yg = lin[(mu_y - 1.0).astype(jnp.int32)]
            return (mu_xg, mu_yg)

        def _get_mask(x, mask_weight, filt):
            bs, depth, h, w = x.shape
            mu_x, mu_y = _get_mu(x)
            posX = jnp.linspace(-1.0, 1.0, h, dtype=x.dtype).reshape(1, 1, h, 1)
            posY = jnp.linspace(-1.0, 1.0, w, dtype=x.dtype).reshape(1, 1, 1, w)
            m = jnp.abs(posX - mu_x[:, :, None, None]) + jnp.abs(posY - mu_y[:, :, None, None])
            m = 1.0 - m * mask_weight.reshape(1, depth, 1, 1)
            m = jnp.maximum(m, -1.0)
            m = jnp.where(filt.reshape(1, depth, 1, 1) == 1.0, m, 1.0)
            return m
        mask = _get_mask(x, mask_weight, filter)
        x_relu = jnp.maximum(x * mask, 0.0)
        out = lax.conv_general_dilated(x_relu, weight, window_strides=(1, 1), padding=[(padding, padding), (padding, padding)], dimension_numbers=('NCHW', 'OIHW', 'NCHW'))
        return out + bias.reshape(1, -1, 1, 1)

    def _L1_conv_ref(x, bias, up_filter, down_filter):
        import jax, jax.numpy as jnp
        from jax import lax
        import numpy as np
        UP = 2
        DOWN = 2
        PADDING = (11, 10, 11, 10)
        GAIN = float(np.sqrt(2.0))
        SLOPE = 0.2
        CLAMP = 256.0
        UP_TAPS = 12
        IN_CUTOFF = 8.0
        OUT_CUTOFF = 8.0
        IN_HALF_WIDTH = 6.0
        OUT_HALF_WIDTH = 6.0
        TEMP_FS = 32.0

        def _design_lowpass(numtaps, cutoff, width, fs):
            nyq = fs / 2.0
            atten = 2.285 * (numtaps - 1) * np.pi * (width / nyq) + 7.95
            if atten > 50.0:
                beta = 0.1102 * (atten - 8.7)
            elif atten > 21.0:
                beta = 0.5842 * (atten - 21.0) ** 0.4 + 0.07886 * (atten - 21.0)
            else:
                beta = 0.0
            m = np.arange(numtaps) - (numtaps - 1) / 2.0
            c = cutoff / nyq
            h = c * np.sinc(c * m)
            h = h * np.kaiser(numtaps, beta)
            h = h / np.sum(h)
            return h.astype(np.float32)

        def _upfirdn2d_sep(x, f, up, down, pad, gain):
            N, C, H, W = x.shape
            fr = f[::-1].astype(x.dtype)
            kH = fr.reshape(1, 1, -1, 1)
            kW = fr.reshape(1, 1, 1, -1)
            px0, px1, py0, py1 = pad
            xr = x.reshape(N * C, 1, H, W)
            xr = lax.conv_general_dilated(xr, kH, window_strides=(down, 1), padding=((py0, py1 + up - 1), (0, 0)), lhs_dilation=(up, 1))
            xr = lax.conv_general_dilated(xr, kW, window_strides=(1, down), padding=((0, 0), (px0, px1 + up - 1)), lhs_dilation=(1, up))
            Ho, Wo = (xr.shape[2], xr.shape[3])
            return xr.reshape(N, C, Ho, Wo) * gain
        y = _upfirdn2d_sep(x, up_filter, UP, 1, PADDING, float(UP * UP))
        y = y + bias[None, :, None, None]
        y = jnp.where(y >= 0, y, y * SLOPE) * GAIN
        y = jnp.clip(y, -CLAMP, CLAMP)
        y = _upfirdn2d_sep(y, down_filter, 1, DOWN, (0, 0, 0, 0), 1.0)
        return y

    def _L2_conv_ref(input_f, in_w, in_b, c1_w, c1_b, c2_w, c2_b, c3_w, c3_b, out_w, out_b, xw1, dtw1, dtb1, Al1, Dv1, g1, be1, xw2, dtw2, dtb2, Al2, Dv2, g2, be2, xw3, dtw3, dtb3, Al3, Dv3, g3, be3):
        import jax, jax.numpy as jnp
        from jax import lax
        import numpy as np
        D_IN = 256
        HID = 64
        D_INNER = 2 * HID
        D_PROJ = 2 * D_INNER
        N_STATE = 16
        R_DT = 8
        B, H, W = (8, 32, 32)

        def _layernorm(y, g, b):
            mu = y.mean(-1, keepdims=True)
            var = ((y - mu) ** 2).mean(-1, keepdims=True)
            return (y - mu) / jnp.sqrt(var + 1e-05) * g + b

        def _ssm(x, xw, dtw, dtb, Al, Dv, g, be):
            Bb, D, L = x.shape
            n = Al.shape[1]
            xd = jnp.einsum('bdl,kd->blk', x, xw)
            dts = xd[..., :R_DT]
            Bs = xd[..., R_DT:R_DT + n]
            Cs = xd[..., R_DT + n:]
            delta = jax.nn.softplus(jnp.einsum('blr,dr->bld', dts, dtw) + dtb)
            A = -jnp.exp(Al)
            xt = x.transpose(0, 2, 1)
            dA = jnp.exp(delta[..., None] * A)
            dBx = delta[..., None] * Bs[:, :, None, :] * xt[..., None]

            def step(h, inp):
                da, dbx, c = inp
                h = h * da + dbx
                return (h, jnp.einsum('bdn,bn->bd', h, c))
            h0 = jnp.zeros((Bb, D, n), x.dtype)
            _, ys = lax.scan(step, h0, (dA.transpose(1, 0, 2, 3), dBx.transpose(1, 0, 2, 3), Cs.transpose(1, 0, 2)))
            y = ys.transpose(1, 0, 2) + xt * Dv
            return _layernorm(y, g, be)

        def _up2(y, h, w):
            Bb, L, C = y.shape
            img = y.transpose(0, 2, 1).reshape(Bb, C, h, w)
            img = jnp.repeat(jnp.repeat(img, 2, axis=2), 2, axis=3)
            return img.reshape(Bb, C, 4 * L).transpose(0, 2, 1)

        def _conv1x1(x, w, b):
            return jnp.einsum('bchw,oc->bohw', x, w) + b[None, :, None, None]

        def _conv2s2(x, w, b):
            out = lax.conv_general_dilated(x, w, (2, 2), 'VALID', dimension_numbers=('NCHW', 'OIHW', 'NCHW'))
            return out + b[None, :, None, None]

        def _forward(input_f, in_w, in_b, c1_w, c1_b, c2_w, c2_b, c3_w, c3_b, out_w, out_b, xw1, dtw1, dtb1, Al1, Dv1, g1, be1, xw2, dtw2, dtb2, Al2, Dv2, g2, be2, xw3, dtw3, dtb3, Al3, Dv3, g3, be3):
            xz = _conv1x1(input_f, in_w, in_b)
            x, z = jnp.split(xz, 2, axis=1)
            f1 = _conv1x1(x, c1_w, c1_b)
            f2 = _conv2s2(f1, c2_w, c2_b)
            f3 = _conv2s2(f2, c3_w, c3_b)
            Bb, C, h3, w3 = f3.shape
            fx3 = f3.reshape(Bb, C, h3 * w3)
            y3 = _ssm(fx3, xw3, dtw3, dtb3, Al3, Dv3, g3, be3) + jnp.flip(_ssm(jnp.flip(fx3, -1), xw3, dtw3, dtb3, Al3, Dv3, g3, be3), 1)
            y2_ = _up2(y3, h3, w3)
            _, _, h2, w2 = f2.shape
            fx2 = f2.reshape(Bb, C, h2 * w2)
            y2 = _ssm(fx2, xw2, dtw2, dtb2, Al2, Dv2, g2, be2) + jnp.flip(_ssm(jnp.flip(fx2, -1), xw2, dtw2, dtb2, Al2, Dv2, g2, be2), 1) + y2_
            y1_ = _up2(y2, h2, w2)
            _, _, h1, w1 = f1.shape
            fx1 = f1.reshape(Bb, C, h1 * w1)
            y1 = _ssm(fx1, xw1, dtw1, dtb1, Al1, Dv1, g1, be1) + jnp.flip(_ssm(jnp.flip(fx1, -1), xw2, dtw2, dtb2, Al2, Dv2, g2, be2), 1) + y1_
            out1 = y1.transpose(0, 2, 1).reshape(Bb, C, h1, w1)
            out = out1 * jax.nn.silu(z)
            return _conv1x1(out, out_w, out_b)
        return _forward(input_f, in_w, in_b, c1_w, c1_b, c2_w, c2_b, c3_w, c3_b, out_w, out_b, xw1, dtw1, dtb1, Al1, Dv1, g1, be1, xw2, dtw2, dtb2, Al2, Dv2, g2, be2, xw3, dtw3, dtb3, Al3, Dv3, g3, be3)

    def _L3_conv_ref(x, bias, up_filter, down_filter):
        import jax, jax.numpy as jnp
        from jax import lax
        import numpy as np
        UP = 2
        DOWN = 2
        PADDING = (11, 10, 11, 10)
        GAIN = float(np.sqrt(2.0))
        SLOPE = 0.2
        CLAMP = 256.0
        UP_TAPS = 12
        IN_CUTOFF = 8.0
        OUT_CUTOFF = 8.0
        IN_HALF_WIDTH = 6.0
        OUT_HALF_WIDTH = 6.0
        TEMP_FS = 32.0

        def _design_lowpass(numtaps, cutoff, width, fs):
            nyq = fs / 2.0
            atten = 2.285 * (numtaps - 1) * np.pi * (width / nyq) + 7.95
            if atten > 50.0:
                beta = 0.1102 * (atten - 8.7)
            elif atten > 21.0:
                beta = 0.5842 * (atten - 21.0) ** 0.4 + 0.07886 * (atten - 21.0)
            else:
                beta = 0.0
            m = np.arange(numtaps) - (numtaps - 1) / 2.0
            c = cutoff / nyq
            h = c * np.sinc(c * m)
            h = h * np.kaiser(numtaps, beta)
            h = h / np.sum(h)
            return h.astype(np.float32)

        def _upfirdn2d_sep(x, f, up, down, pad, gain):
            N, C, H, W = x.shape
            fr = f[::-1].astype(x.dtype)
            kH = fr.reshape(1, 1, -1, 1)
            kW = fr.reshape(1, 1, 1, -1)
            px0, px1, py0, py1 = pad
            xr = x.reshape(N * C, 1, H, W)
            xr = lax.conv_general_dilated(xr, kH, window_strides=(down, 1), padding=((py0, py1 + up - 1), (0, 0)), lhs_dilation=(up, 1))
            xr = lax.conv_general_dilated(xr, kW, window_strides=(1, down), padding=((0, 0), (px0, px1 + up - 1)), lhs_dilation=(1, up))
            Ho, Wo = (xr.shape[2], xr.shape[3])
            return xr.reshape(N, C, Ho, Wo) * gain
        y = _upfirdn2d_sep(x, up_filter, UP, 1, PADDING, float(UP * UP))
        y = y + bias[None, :, None, None]
        y = jnp.where(y >= 0, y, y * SLOPE) * GAIN
        y = jnp.clip(y, -CLAMP, CLAMP)
        y = _upfirdn2d_sep(y, down_filter, 1, DOWN, (0, 0, 0, 0), 1.0)
        return y

    def _gn(v, G=32, eps=1e-05):
        B_, C_, H_, W_ = v.shape
        g = v.reshape(B_, G, C_ // G, H_, W_)
        m = jnp.mean(g, axis=(2, 3, 4), keepdims=True)
        s = jnp.var(g, axis=(2, 3, 4), keepdims=True)
        return ((g - m) / jnp.sqrt(s + eps)).reshape(v.shape)

    def _ln_c(v, eps=1e-06):
        m = jnp.mean(v, axis=1, keepdims=True)
        s = jnp.var(v, axis=1, keepdims=True)
        return (v - m) / jnp.sqrt(s + eps)

    def _ln_t(v, eps=1e-05):
        m = jnp.mean(v, axis=-1, keepdims=True)
        s = jnp.var(v, axis=-1, keepdims=True)
        return (v - m) / jnp.sqrt(s + eps)

    def _to_tokens(v):
        B_, C_, H_, W_ = v.shape
        return v.reshape(B_, C_, H_ * W_).transpose(0, 2, 1)

    def _from_tokens(t, like):
        B_, C_, H_, W_ = like.shape
        return t.transpose(0, 2, 1).reshape(B_, C_, H_, W_)
    x = x + _L0_conv_ref(_gn(x), L0_conv_weight, L0_conv_bias, L0_conv_mask_weight, L0_conv_filter, 1)
    x = x + _L1_conv_ref(_gn(x), L1_conv_bias, L1_conv_up_filter, L1_conv_down_filter)
    x = x + _L2_conv_ref(_gn(x), L2_conv_in_w, L2_conv_in_b, L2_conv_c1_w, L2_conv_c1_b, L2_conv_c2_w, L2_conv_c2_b, L2_conv_c3_w, L2_conv_c3_b, L2_conv_out_w, L2_conv_out_b, L2_conv_xw1, L2_conv_dtw1, L2_conv_dtb1, L2_conv_Al1, L2_conv_Dv1, L2_conv_g1, L2_conv_be1, L2_conv_xw2, L2_conv_dtw2, L2_conv_dtb2, L2_conv_Al2, L2_conv_Dv2, L2_conv_g2, L2_conv_be2, L2_conv_xw3, L2_conv_dtw3, L2_conv_dtb3, L2_conv_Al3, L2_conv_Dv3, L2_conv_g3, L2_conv_be3)
    x = x + _L3_conv_ref(_gn(x), L3_conv_bias, L3_conv_up_filter, L3_conv_down_filter)
    return x

_drawn_inputs = setup_inputs


def setup_inputs(seed=0):
    import zlib

    import numpy as np

    out = dict(_drawn_inputs(seed))
    spreads = {'L0_conv_filter': (1.0, 0.2),
     'L2_conv_Dv1': (1.0, 0.6),
     'L2_conv_g1': (1.0, 0.6),
     'L2_conv_be1': (0.0, 0.62),
     'L2_conv_Dv2': (1.0, 0.6),
     'L2_conv_g2': (1.0, 0.2),
     'L2_conv_be2': (0.0, 0.1),
     'L2_conv_Dv3': (1.0, 0.6),
     'L2_conv_g3': (1.0, 0.2),
     'L2_conv_be3': (0.0, 0.328)}
    factors = {'L2_conv_xw1': 8.0,
     'L2_conv_dtw1': 8.0,
     'L2_conv_dtb1': 34.858,
     'L2_conv_Al1': 8.0,
     'L2_conv_xw2': 8.0,
     'L2_conv_dtw2': 8.0,
     'L2_conv_dtb2': 23.604,
     'L2_conv_Al2': 8.0,
     'L2_conv_xw3': 8.0,
     'L2_conv_dtw3': 8.0,
     'L2_conv_dtb3': 34.29,
     'L2_conv_Al3': 8.0}
    for name, (base, spread) in spreads.items():
        noise = np.random.default_rng([zlib.crc32(name.encode()), seed]).standard_normal(out[name].shape)
        drawn = base * np.exp(spread * noise) if base else spread * noise
        out[name] = jnp.asarray(drawn.astype(out[name].dtype))
    for name, factor in factors.items():
        out[name] = (out[name] * factor).astype(out[name].dtype)
    return out
```

```python
from contextlib import ExitStack

import concourse.bass as bass
from concourse import mybir

F32 = mybir.dt.float32
BF16 = mybir.dt.bfloat16
ALU = mybir.AluOpType
ACT = mybir.ActivationFunctionType
AX = mybir.AxisListType.X

P = 128
N_SAMPLES, CH, HH, WW = 32, 256, 28, 28
HW = HH * WW
NC = CH // P
HALF = HW // 2
GROUP = 8
GN_EPS = 1e-5
LN_EPS = 1e-5
MAGIC = 12582912.0
SERIES_UNTIL = 2.0 ** -6
STEP = 2.0 / (HH - 1)

TILE = 11
KP = TILE * TILE
PATCH0 = [0, 6, 11, 17]
TYPE_TILES = [[0], [1, 3], [2, 4], [5]]
TYPE_PATCHES = [[0], [0, 2], [1, 3], [3]]
TILE_PATCH = [0, 0, 1, 2, 3, 3]
TILE_ROWS = [(0, 6), (0, 11), (0, 11), (0, 11), (0, 11), (5, 11)]
SPLIT = 17
UP_STEPS = ([[(a, b)] for a in (1, 2) for b in (1, 2)]
            + [[(a, 1), (a, 2)] for a in (0, 3)] + [[(1, b), (2, b)] for b in (0, 3)]
            + [[(0, 0), (0, 3), (3, 0), (3, 3)]])
N_UP = len(UP_STEPS)
SQRT2 = 2.0 ** 0.5
CLAMP = 256.0
SLOPE = 0.2

N_STATE = 16
R_DT = 8
LEN = [HW, HW // 4, HW // 16]
BRANCH = [(2, 2), (1, 1), (0, 0), (0, 1)]
PER_STEP = [1, 4, 16]
SCAN_STEPS = [(q, g) for q, (lev, _) in enumerate(BRANCH) for g in range(N_STATE // PER_STEP[lev])]
SCANS = [(k, q, g, d) for k, (q, g) in enumerate(SCAN_STEPS)
         for d in ((0, 1) if BRANCH[q][0] else ((0,) if q == 2 else (1,)))]
POOL_ADDS = [j for j, (k, q, g, d) in enumerate(SCANS) if g > 0]
LAST_SCAN = {k: j for j, (k, q, g, d) in enumerate(SCANS)}
SCANS_OF = {k: [j for j, s in enumerate(SCANS) if s[0] == k] for k in range(len(SCAN_STEPS))}
NORMS = [0, 1, 2, 3]


def scan_layer_order():
    order = [("b_gn",), ("b_in", 0), ("b_in", 1), ("b_f1",), ("b_f2",), ("b_f3",)]
    for q in (0, 1):
        order += [("prep", q), ("split", q), ("delta", q)]
    order += [("cast_b", 0), ("dbx", 0)]
    between = {1: [("split", 2)], 2: [("delta", 2)], 3: [("split", 3)], 4: [("delta", 3)],
               5: [("fold", 1)], 6: [("y", 0)], 7: [("centre", 0)], 9: [("mix", 0), ("y", 1)], 10: [("centre", 1)],
               12: [("mix", 1)], 22: [("y", 2)], 23: [("centre", 2)], 25: [("mix", 2)]}
    ahead = {0: [("fold", 0), ("prep", 2)], 2: [("prep", 3)], 6: [("mean", 0)], 7: [("var", 0)], 9: [("mean", 1)],
             10: [("var", 1)], 22: [("mean", 2)], 23: [("var", 2)]}
    for k in range(len(SCAN_STEPS)):
        following = [("cast_b", k + 1), ("dbx", k + 1)] if k + 1 < len(SCAN_STEPS) else []
        order += [("scan", k)] + between.get(k, []) + [("cast_c", k)]
        if k in ahead:
            order += [("hc", k)] + ahead[k] + following
        else:
            order += following + [("hc", k)]
    order += [("y", 3), ("mean", 3), ("centre", 3), ("var", 3), ("mix", 3), ("gate",), ("b_out", 0), ("b_out", 1)]
    return order


def slot_uses(order):
    names = []
    for kind, *a in order:
        if kind in ("b_in", "b_out"):
            names.append((kind, a[0]))
        elif kind in ("b_f1", "b_f2", "b_f3"):
            names.append((kind, 0))
        elif kind == "prep":
            names += [("V", a[0]), ("BC", a[0])]
        elif kind == "cast_b":
            names.append(("B", a[0]))
        elif kind == "cast_c":
            names.append(("C", a[0]))
        elif kind in ("mean", "var"):
            names.append((kind, a[0]))
    return {n: i for i, n in enumerate(names)}


def filter_order(p):
    out = []
    for c in range(NC):
        out += [("turn", p, c, k) for k in range(4)]
        for u in range(N_UP + 2):
            if u < N_UP:
                out.append(("up", p, c, u))
            if u >= 2:
                out.append(("down", p, c, u - 2))
        out.append(("fin", p, c))
    return out


def merge(a, b):
    out, i, j = [], 0, 0
    while i < len(a) or j < len(b):
        if j >= len(b) or (i < len(a) and i * len(b) <= j * len(a)):
            out.append(a[i])
            i += 1
        else:
            out.append(b[j])
            j += 1
    return out


def build(nc, t):
    ctx = ExitStack()
    with ctx:
        def sb(name, shape, dt=F32):
            return ctx.enter_context(nc.sbuf_tensor(name, shape, dt))

        SEMS = []

        def sem(name):
            s = ctx.enter_context(nc.semaphore(name))
            SEMS.append(s)
            return s

        ident = sb("ident", [P, P])
        group_mean = sb("group_mean", [P, P])
        chan_mean = sb("chan_mean", [P, P])
        pick = sb("pick", [P, 2 * N_STATE])
        pick_bf = sb("pick_bf", [P, 2 * N_STATE], BF16)
        ramp = sb("ramp", [P, 4, HH])
        grid = sb("grid", [P, HH])
        conv_w = sb("conv_w", [P, NC, 9, CH])
        conv_b = sb("conv_b", [P, NC])
        neg_mw = sb("neg_mw", [P, NC])
        filt = sb("filt", [P, NC])
        up_k = [sb(f"up_k{l}", [P, 16, KP]) for l in range(2)]
        down_k = [sb(f"down_k{l}", [P, 16, TILE, TILE]) for l in range(2)]
        in_w = sb("in_w", [P, NC, CH])
        in_b = sb("in_b", [P, 2])
        c1_w = sb("c1_w", [P, P])
        c23_w = sb("c23_w", [P, 2, 4, P])
        c_b = sb("c_b", [P, 3])
        out_w = sb("out_w", [P, CH])
        out_b = sb("out_b", [P, NC])
        bc_w = sb("bc_w", [P, 3, 4, 2 * N_STATE])
        dt_w = sb("dt_w", [P, 3, P])
        dt_b = sb("dt_b", [P, 3])
        a_neg = sb("a_neg", [P, 3, N_STATE])
        dv = sb("dv", [P, 3])
        ln_g = sb("ln_g", [P, 3])
        ln_b = sb("ln_b", [P, 3])
        bias_sum = sb("bias_sum", [P, 1])
        eps = sb("eps", [P, 2])

        xa = sb("xa", [P, NC, HW])
        xp = sb("xp", [P, NC, 4, HH * TILE])
        xg = xp[:, :, :, :].rearrange("p c j n -> p c (j n)")[:, :, 0:HW]
        x2 = sb("x2", [P, NC, HW])
        x3 = sb("x3", [P, NC, HW])
        pad = sb("pad", [P, NC, HH + 2, WW + 2])
        msk = sb("msk", [P, HW])
        xt = sb("xt", [P, NC, 16, P])
        NY = 4
        ys = sb("ys", [P, NY, 4 * P])
        d_a0 = sb("d_a0", [P, 2, HW])
        d_b0 = sb("d_b0", [P, 2, HW])
        d_a1 = sb("d_a1", [P, 4, LEN[1] + 1])
        d_b1 = sb("d_b1", [P, 4, LEN[1] + 1])
        d_a2 = sb("d_a2", [P, 16, LEN[2] + 1])
        d_b2 = sb("d_b2", [P, 16, LEN[2] + 1])
        NH = 3
        hs = sb("hs", [P, NH, 16 * (LEN[2] + 1)])
        acc = sb("acc", [P, 2, HW])
        f1 = sb("f1", [P, HW])
        f2 = sb("f2", [P, LEN[1]])
        f3 = sb("f3", [P, LEN[2]])
        zs = sb("zs", [P, HW])
        sz = sb("sz", [P, HW])
        delta = sb("delta", [P, sum(LEN) + HW])
        dx = sb("dx", [P, sum(LEN) + HW])
        bct = sb("bct", [P, sum(LEN) + HW], BF16)
        va = sb("va", [P, HW])
        vb = sb("vb", [P, HW])
        vc = sb("vc", [P, HW])
        y1 = sb("y1", [P, HW])
        y2 = sb("y2", [P, LEN[1]])
        y3 = sb("y3", [P, LEN[2]])
        sums3 = sb("sums3", [P, 2 * LEN[2]])
        g2 = d_a0
        poly, far = d_b0[:, 0, :], d_b0[:, 1, :]
        xs = rest = y1
        st = [sb(f"st{i}", [P, NC, 2, 6]) for i in range(2)]
        mv = [sb(f"mv{i}", [P, NC, 2]) for i in range(2)]
        dev = [sb(f"dev{i}", [P, 3, NC]) for i in range(2)]
        rstd = [sb(f"rstd{i}", [P, NC]) for i in range(2)]
        lnv = [sb(f"lnv{i}", [P, NC]) for i in range(2)]
        nbias = [sb(f"nbias{i}", [P, NC]) for i in range(2)]
        lines = sb("lines", [P, 2, NC, HH])
        wlines = sb("wlines", [P, 2, NC, HH])
        s0 = sb("s0", [P, 2, NC])
        s1 = sb("s1", [P, 2, NC])
        cen = sb("cen", [P, 5, 2 * NC])
        dist = sb("dist", [P, 2, NC, HH])
        ahbw = sb("ahbw", [P, 2, NC, HH])

        ps = ctx.enter_context(nc.psum_tensor("ps", [P, 8, 512], F32))

        F = [f1, f2, f3]
        OFF = [LEN[0] * 2 + LEN[1], LEN[0] * 2, 0, LEN[0]]

        def part(buf, q):
            n = LEN[BRANCH[q][0]]
            return buf[:, OFF[q]:OFF[q] + n]

        def img(ap, n=HH):
            return ap.rearrange("p (h w) -> p h w", w=n)

        s_load = sem("s_load")
        s_stage = sem("s_stage")
        s_kron = sem("s_kron")
        s_set = sem("s_set")
        s_comb = sem("s_comb")
        s_zero = sem("s_zero")
        s_exp = sem("s_exp")
        stage = [d_a0[:, :, :].rearrange("p a b -> p (a b)")[:, 0:4 * KP], d_b0[:, :, :].rearrange("p a b -> p (a b)")[:, 0:4 * KP]]
        raw_dt = va[0:R_DT, :]
        loads = [
            (ident[:, :], t["ident"]), (group_mean[:, :], t["group_mean"]), (chan_mean[:, :], t["chan_mean"]),
            (pick[:, :], t["pick"]), (ramp[:, :, :], t["ramp"]), (grid[:, :], t["grid"]),
            (conv_w[:, :, :, :], t["conv_w"]), (conv_b[:, :], t["conv_b"]), (neg_mw[:, :], t["mask_w"]),
            (filt[:, :], t["filt"]), (in_w[:, :, :], t["in_w"]), (in_b[:, :], t["in_b"]), (c1_w[:, :], t["c1_w"]),
            (c23_w[:, :, :, :], t["c23_w"]), (c_b[:, :], t["c_b"]), (out_w[:, :], t["out_w"]), (out_b[:, :], t["out_b"]),
            (bc_w[:, :, :, :], t["bc_w"]), (dt_b[:, :], t["dt_b"]), (a_neg[:, :, :], t["al"]), (dv[:, :], t["dv"]),
            (ln_g[:, :], t["ln_g"]), (ln_b[:, :], t["ln_b"]), (raw_dt[:, 0:6 * P], t["dt_parts"]),
            (up_k[0][KP:KP + 2, :, :], t["bias_on"][0]), (up_k[1][KP:KP + 2, :, :], t["bias_on"][1]),
            (xt[KP:KP + 2, :, :, :], t["bias_rows"]),
        ]
        with nc.Block() as block:
            @block.sync
            def _(sp):
                for dst, src in loads:
                    sp.dma_start(dst, src).then_inc(s_load, 16)
                for n in range(4):
                    if n:
                        sp.wait_ge(s_kron, 16 * n)
                    for a in range(2):
                        sp.dma_start(stage[a][0:KP, :], t["taps"][n, a]).then_inc(s_stage, 16)

            @block.vector
            def _(dve):
                for n in range(4):
                    dve.wait_ge(s_stage, 32 * (n + 1))
                    k = (up_k[n // 2] if n % 2 == 0 else
                         down_k[n // 2][:, :, :, :].rearrange("p k a b -> p k (a b)"))
                    for a in range(4):
                        for b in range(4):
                            nc.vector.scalar_tensor_tensor(
                                out=k[0:KP, 4 * a + b, :], in0=stage[0][0:KP, a * KP:(a + 1) * KP],
                                scalar=4.0 * SQRT2 if n % 2 == 0 else 1.0,
                                in1=stage[1][0:KP, b * KP:(b + 1) * KP],
                                op0=ALU.mult, op1=ALU.mult).then_inc(s_kron, 1)
                dve.wait_ge(s_load, 16 * len(loads))
                nc.vector.tensor_copy(pick_bf[:, :], pick[:, :]).then_inc(s_set, 1)
                nc.vector.tensor_scalar(filt[:, :], filt[:, :], 1.0, -1.0, ALU.is_equal, ALU.mult).then_inc(s_set, 1)
                dve.wait_ge(s_set, 2)
                nc.vector.tensor_tensor(neg_mw[:, :], neg_mw[:, :], filt[:, :], ALU.mult).then_inc(s_set, 1)
                nc.vector.tensor_scalar(bias_sum[:, :], ln_b[:, 1:2], 3.0, ln_b[:, 0:1], ALU.mult, ALU.add).then_inc(s_set, 1)
                dve.wait_ge(s_set, 4)
                nc.vector.scalar_tensor_tensor(out=bias_sum[:, :], in0=ln_b[:, 2:3], scalar=2.0, in1=bias_sum[:, :],
                                               op0=ALU.mult, op1=ALU.add).then_inc(s_set, 1)
                dve.wait_ge(s_exp, 1)
                nc.vector.tensor_scalar(a_neg[:, :, :], a_neg[:, :, :], -1.0, None, ALU.mult).then_inc(s_set, 1)
                dve.wait_ge(s_comb, 3)
                nc.vector.tensor_copy(dt_w[:, :, :], ps[:, 0, 0:3 * P]).then_inc(s_set, 1)
                nc.vector.memset(eps[:, 0:1], GN_EPS).then_inc(s_set, 1)
                nc.vector.memset(eps[:, 1:2], LN_EPS).then_inc(s_set, 1)

            @block.gpsimd
            def _(pool):
                for buf in (pad[:, :, :, :], d_a1[:, :, :], d_b1[:, :, :], d_a2[:, :, :], d_b2[:, :, :]):
                    nc.gpsimd.memset(buf, 0.0).then_inc(s_zero, 1)

            @block.scalar
            def _(act):
                nc.scalar.preload_act_table_set("natural_log_exp_and_others")
                act.wait_ge(s_load, 16 * len(loads))
                nc.scalar.activation(a_neg[:, :, :], a_neg[:, :, :], ACT.Exp).then_inc(s_exp, 1)

            @block.tensor
            def _(pe):
                pe.wait_ge(s_load, 16 * len(loads))
                for w in range(3):
                    nc.tensor.matmul(ps[:, 0, w * P:(w + 1) * P], raw_dt[:, 2 * w * P:(2 * w + 1) * P],
                                     raw_dt[:, (2 * w + 1) * P:(2 * w + 2) * P], start=True, stop=True).then_inc(s_comb, 1)

        b_order = scan_layer_order()
        USE = slot_uses(b_order)

        x_loaded = sem("x_loaded")
        y_stored = sem("y_stored")
        gn_vec = [sem("xgn_vec"), sem("bgn_vec")]
        gn_mm = [sem("xgn_mm"), sem("bgn_mm")]
        gn_act = [sem("xgn_act"), sem("bgn_act")]
        mask_vec = sem("mask_vec")
        mask_dist = sem("mask_dist")
        relu_done = sem("relu_done")
        conv_sum = sem("conv_sum")
        conv_added = sem("conv_added")
        turned = sem("turned")
        turn_copied = sem("turn_copied")
        up_sum = sem("up_sum")
        up_relu = sem("up_relu")
        up_leaky = sem("up_leaky")
        up_clipped = sem("up_clipped")
        down_sum = sem("down_sum")
        layer_added = sem("layer_added")
        x2_copied = sem("x2_copied")
        slot_full = sem("slot_full")
        b_copied = sem("b_copied")
        gate_z = sem("gate_z")
        gate_exp = sem("gate_exp")
        gate_fin = sem("gate_fin")
        gate_mul = sem("gate_mul")
        v_act = sem("v_act")
        v_pool = sem("v_pool")
        v_series = sem("v_series")
        v_log = sem("v_log")
        delta_done = sem("delta_done")
        dx_done = sem("dx_done")
        hi_done = sem("hi_done")
        rest_done = sem("rest_done")
        mid_done = sem("mid_done")
        bct_done = sem("bct_done")
        da_done = sem("da_done")
        dbx_done = sem("dbx_done")
        scan_done = sem("scan_done")
        hc_done = sem("hc_done")
        state_added = sem("state_added")
        fold_done = sem("fold_done")
        y_done = sem("y_done")
        centred = sem("centred")
        squared = sem("squared")
        ln_rstd = sem("ln_rstd")
        y_normed = sem("y_normed")
        y_mixed = sem("y_mixed")
        gated = sem("gated")
        x3_done = sem("x3_done")
        turn_sems = SEMS[7:]

        POOL_COUNT = {j: i + 1 for i, j in enumerate(POOL_ADDS)}

        def pool_adds_before(j):
            return sum(1 for a in POOL_ADDS if a < j)

        def slot(name):
            return ps[:, 4 + 2 * (USE[name] % 2):6 + 2 * (USE[name] % 2), :]

        def release(name):
            kind, i = name
            return {"b_in": (b_copied, i + 1), "b_f1": (b_copied, 3), "b_f2": (b_copied, 4), "b_f3": (b_copied, 5),
                    "V": (v_act, 4 * i + 1), "BC": (rest_done, i + 1), "B": (dbx_done, i + 1),
                    "C": (hc_done, LAST_SCAN.get(i, 0) + 1), "mean": (centred, i + 1),
                    "var": (ln_rstd, 2 * i + 1), "b_out": (x3_done, i + 1)}[kind]

        NAME_AT = {i: n for n, i in USE.items()}

        def full(name):
            return USE[name] + 1

        ADD_STEPS = {0: 1, 1: 3, 2: 3, 3: 2}

        def mixed_until(q):
            return sum(ADD_STEPS[i] for i in range(q))

        def da_view(k):
            q, g = SCAN_STEPS[k]
            return {0: d_a0[:, k % 2, :], 1: d_a1, 2: d_a2}[BRANCH[q][0]]

        def db_view(k):
            q, g = SCAN_STEPS[k]
            return {0: d_b0[:, k % 2, :], 1: d_b1, 2: d_b2}[BRANCH[q][0]]

        def h_view(j):
            lev = BRANCH[SCANS[j][1]][0]
            if lev == 0:
                return hs[:, j % NH, 0:HW]
            n = LEN[lev] + 1
            return hs[:, j % NH, 0:PER_STEP[lev] * n].rearrange("p (n l) -> p n l", l=n)

        def turn(block, has_b, has_last, has_first, load_at, store_at):
            passes = (["last"] if has_last else []) + (["first"] if has_first else [])
            LAY = {"last": 1, "first": 0}
            x_order = []
            inst = {}
            if has_last:
                inst["last"] = 0
                x_order += [("x_gn", "last")] + filter_order(0)
            if has_b:
                x_order.append(("keep",))
            if has_first:
                inst["conv"] = len(inst)
                inst["first"] = len(inst)
                x_order += [("x_gn", "conv"), ("mask",)] + [("conv", g) for g in range(4)]
                x_order += [("x_gn", "first")] + filter_order(passes.index("first"))
            order = merge(b_order if has_b else [], x_order)
            SRC = {"last": x3, "conv": xa, "first": xa}
            ACT_BASE, at = {}, 0
            for which in inst:
                ACT_BASE[which] = at
                at += 4 if which == "conv" else 10

            def normed(which, c):
                return ACT_BASE[which] + 2 + (c + 1) * (1 if which == "conv" else 4)

            def norm_width(q):
                lev = BRANCH[q][0]
                return LEN[lev] * (2 if lev else 1)

            def ring(p, c, k):
                return (2 * p + c) * (4 + N_UP) + k

            def bank(r):
                return ps[:, 2 + r % 2, :]

            def wait_bank(pe, r):
                if r >= 2:
                    pc, k = divmod(r - 2, 4 + N_UP)
                    if k < 4:
                        pe.wait_ge(turn_copied, 4 * pc + k + 1)
                    else:
                        pe.wait_ge(up_leaky, N_UP * pc + k - 4 + 1)

            def up_groups(u):
                at = 0
                for a, b in UP_STEPS[u]:
                    tiles = [(i, j) for i in TYPE_TILES[a] for j in TYPE_TILES[b]]
                    yield a, b, at, tiles
                    at += len(tiles) * P

            @block.sync
            def _(sp):
                if has_first:
                    sp.dma_start(xa[:, :, :], load_at).then_inc(x_loaded, 16)
                if has_last:
                    sp.wait_ge(layer_added, 4)
                    sp.dma_start(store_at, xg[:, :, :]).then_inc(y_stored, 16)
                    sp.wait_ge(y_stored, 16)

            @block.tensor
            def _(pe):
                def gn(x, i):
                    pe.wait_ge(gn_vec[x], 10 * i + 6)
                    at = (ps[:, 0, 496:500] if x == 0 else ps[:, 4, 496:500])
                    if x == 0 and i:
                        if has_last:
                            pe.wait_ge(layer_added, 4)
                        if i == inst.get("first"):
                            pe.wait_ge(conv_added, 4)
                    nc.tensor.matmul(at[:, 0:2], group_mean[:, :], mv[x][:, :, 0], start=True, stop=True).then_inc(gn_mm[x], 1)
                    pe.wait_ge(gn_vec[x], 10 * i + 9)
                    nc.tensor.matmul(at[:, 2:4], group_mean[:, :], dev[x][:, 2, :], start=True, stop=True).then_inc(gn_mm[x], 1)

                def x_gn(which):
                    gn(0, inst[which])

                def conv(g):
                    m, half = divmod(g, 2)
                    if g == 0:
                        pe.wait_ge(gn_vec[0], 10 * inst["conv"] + 10)
                    if g >= 2:
                        pe.wait_ge(conv_added, g - 1)
                    for c in range(NC):
                        pe.wait_ge(relu_done, c + 1)
                        for tap in range(9):
                            r0 = half * (HH // 2) + tap // 3
                            mm = nc.tensor.matmul(ps[:, half, 0:HALF], conv_w[:, c, tap, m * P:(m + 1) * P],
                                                  pad[:, c, r0:r0 + HH // 2, tap % 3:tap % 3 + WW],
                                                  start=(c == 0 and tap == 0), stop=(c == NC - 1 and tap == 8))
                    mm.then_inc(conv_sum, 1)

                def turn_patches(p, c, k):
                    pe.wait_ge(gn_act[0], normed(passes[p], c))
                    wait_bank(pe, ring(p, c, k))
                    out = bank(ring(p, c, k))
                    for j in range(4):
                        h0 = PATCH0[k]
                        mm = nc.tensor.transpose(out[0:KP, j * P:(j + 1) * P],
                                                 xp[:, c, j, h0 * TILE:(h0 + TILE) * TILE], ident[:, :])
                    mm.then_inc(turned, 1)

                def up(p, c, u):
                    pe.wait_ge(turn_copied, 4 * (2 * p + c) + 4)
                    wait_bank(pe, ring(p, c, 4 + u))
                    out = bank(ring(p, c, 4 + u))
                    for a, b, at, tiles in up_groups(u):
                        pa, pb = TYPE_PATCHES[a], TYPE_PATCHES[b]
                        x16 = xt[:, c, :, :].rearrange("p (i j) n -> p i j n", j=4)
                        mm = nc.tensor.matmul(out[0:KP, at:at + len(tiles) * P],
                                              up_k[LAY[passes[p]]][0:KP + 2, 4 * a + b, :],
                                              x16[0:KP + 2, pa[0]:pa[-1] + 1:2, pb[0]:pb[-1] + 1:2, :],
                                              start=True, stop=True)
                    mm.then_inc(up_sum, 1)

                def down(p, c, u):
                    y = N_UP * (2 * p + c) + u
                    pe.wait_ge(up_clipped, y + 1)
                    if u == 0:
                        if 2 * p + c:
                            pe.wait_ge(layer_added, 2 * (2 * p + c))
                        if passes[p] == "first":
                            pe.wait_ge(conv_added, 4)
                        pe.wait_ge(gn_vec[0], 10 * inst[passes[p]] + 10)
                    todo = []
                    for a, b, at, tiles in up_groups(u):
                        for n, (i, j) in enumerate(tiles):
                            r0, r1 = TILE_ROWS[i]
                            base = PATCH0[TILE_PATCH[i]]
                            for lo, hi, reg in ((r0, min(r1, SPLIT - base), 0), (max(r0, SPLIT - base), r1, 1)):
                                if lo < hi:
                                    todo.append((a, b, at + n * P, j, base, lo, hi, reg))
                    for a, b, col, j, base, lo, hi, reg in todo:
                        w0, w1 = TILE_ROWS[j]
                        wb = PATCH0[TILE_PATCH[j]]
                        rows = SPLIT if reg == 0 else HH - SPLIT
                        out = img(ps[:, reg, 0:rows * WW])[:, base + lo - reg * SPLIT:base + hi - reg * SPLIT, wb + w0:wb + w1]
                        mm = nc.tensor.matmul(out, ys[0:KP, y % NY, col:col + P],
                                              down_k[LAY[passes[p]]][0:KP, 4 * a + b, lo:hi, w0:w1],
                                              start=FIRST.pop((p, c, reg), True), stop=(u == N_UP - 1),
                                              skip_group_check=True)
                        FIRST[(p, c, reg)] = False
                    mm.then_inc(down_sum, 1)

                FIRST = {}

                def take(name):
                    i = USE[name]
                    if i >= 2:
                        pe.wait_ge(*release(NAME_AT[i - 2]))
                    return slot(name)

                def in_proj(m):
                    out = take(("b_in", m))
                    for half in range(2):
                        for c in range(NC):
                            pe.wait_ge(gn_act[1], 3 + c)
                            mm = nc.tensor.matmul(out[:, half, 0:HALF], in_w[:, c, m * P:(m + 1) * P],
                                                  g2[:, c, half * HALF:(half + 1) * HALF], start=(c == 0), stop=(c == 1))
                    mm.then_inc(slot_full, 1)

                def b_gn():
                    gn(1, 0)

                def b_in(m):
                    if m == 0:
                        pe.wait_ge(gn_vec[1], 10)
                    in_proj(m)

                def b_f1():
                    out = take(("b_f1", 0))
                    pe.wait_ge(b_copied, 1)
                    for half in range(2):
                        mm = nc.tensor.matmul(out[:, half, 0:HALF], c1_w[:, :], xs[:, half * HALF:(half + 1) * HALF], start=True, stop=True)
                    mm.then_inc(slot_full, 1)

                def shrink(name, src, side, lev, copied):
                    out = take(name)
                    pe.wait_ge(b_copied, copied)
                    v = img(src[:, :], side)
                    for tap in range(4):
                        mm = nc.tensor.matmul(out[:, 0, 0:LEN[lev]], c23_w[:, lev - 1, tap, :],
                                              v[:, tap // 2:side:2, tap % 2:side:2], start=(tap == 0), stop=(tap == 3))
                    mm.then_inc(slot_full, 1)

                def b_f2():
                    shrink(("b_f2", 0), f1, HH, 1, 3)

                def b_f3():
                    shrink(("b_f3", 0), f2, HH // 2, 2, 4)

                def halves(n):
                    return [(0, HALF), (1, HALF)] if n == HW else [(0, n)]

                def prep(q):
                    lev, w = BRANCH[q]
                    pe.wait_ge(b_copied, {0: 3, 1: 4, 2: 5}[lev])
                    for name, wt in (("V", dt_w[:, w, :]), ("BC", bc_w[:, w, :, :])):
                        out = take((name, q))
                        for half, n in halves(LEN[lev]):
                            mm = nc.tensor.matmul(out[:, half, 0:n], wt, F[lev][:, half * HALF:half * HALF + n], start=True, stop=True)
                        mm.then_inc(slot_full, 1)

                def cast(name, base, k):
                    q, g = SCAN_STEPS[k]
                    lev = BRANCH[q][0]
                    pe.wait_ge(bct_done, q + 1)
                    src = part(bct, q)
                    out = take((name, k))
                    if lev == 0:
                        for half in range(2):
                            mm = nc.tensor.matmul(out[:, half, 0:HALF],
                                                  pick_bf[:, base + g:base + g + 1].broadcast_to([P, P]),
                                                  src[:, half * HALF:(half + 1) * HALF], start=True, stop=True)
                    else:
                        n = LEN[lev]
                        per = PER_STEP[lev] // 2
                        for i in range(PER_STEP[lev]):
                            s = base + g * PER_STEP[lev] + i
                            mm = nc.tensor.matmul(out[:, i // per, (i % per) * n:(i % per + 1) * n],
                                                  pick_bf[:, s:s + 1].broadcast_to([P, P]), src, start=True, stop=True)
                    mm.then_inc(slot_full, 1)

                def cast_b(k):
                    cast("B", 0, k)

                def cast_c(k):
                    cast("C", N_STATE, k)

                def average(name, ready, q):
                    out = take((name, q))
                    pe.wait_ge(ready, q + 1)
                    for half, m in halves(norm_width(q)):
                        mm = nc.tensor.matmul(out[:, half, 0:m], chan_mean[:, :], va[:, half * HALF:half * HALF + m], start=True, stop=True)
                    mm.then_inc(slot_full, 1)

                def mean(q):
                    average("mean", y_done, q)

                def var(q):
                    average("var", squared, q)

                def b_out(m):
                    out = take(("b_out", m))
                    pe.wait_ge(gated, 1)
                    for half in range(2):
                        mm = nc.tensor.matmul(out[:, half, 0:HALF], out_w[:, m * P:(m + 1) * P],
                                              y1[:, half * HALF:(half + 1) * HALF], start=True, stop=True)
                    mm.then_inc(slot_full, 1)

                do = {"x_gn": x_gn, "conv": conv, "turn": turn_patches, "up": up, "down": down, "b_gn": b_gn, "b_in": b_in,
                      "b_f1": b_f1, "b_f2": b_f2, "b_f3": b_f3, "prep": prep, "cast_b": cast_b, "cast_c": cast_c, "mean": mean, "var": var, "b_out": b_out}
                for kind, *a in order:
                    if kind in do:
                        do[kind](*a)

            @block.scalar
            def _(act):
                def gn(x, i, base, src, free, parts):
                    at = (ps[:, 0, 496:500] if x == 0 else ps[:, 4, 496:500])
                    act.wait_ge(gn_mm[x], 2 * i + 2)
                    nc.scalar.activation(lnv[x][:, :], at[:, 2:4], ACT.Ln, bias=eps[:, 0:1]).then_inc(gn_act[x], 1)
                    act.wait_ge(gn_act[x], base + 1)
                    nc.scalar.activation(rstd[x][:, :], lnv[x][:, :], ACT.Exp, scale=-0.5).then_inc(gn_act[x], 1)
                    act.wait_ge(gn_vec[x], 10 * i + 10)
                    for s, v in free:
                        act.wait_ge(s, v)
                    for c in range(NC):
                        for dst, part_of in parts(c):
                            nc.scalar.activation(dst, part_of(src), ACT.Identity, bias=nbias[x][:, c:c + 1],
                                                 scale=rstd[x][:, c:c + 1]).then_inc(gn_act[x], 1)

                def x_gn(which):
                    free = {"last": [], "conv": [(y_stored, 16)] if has_last else [],
                            "first": [(mask_vec, 21)]}[which]

                    def parts(c):
                        if which == "conv":
                            return [(xg[:, c, :], lambda v: v[:, c, :])]
                        return [(img(xp[:, c, j, :], TILE), lambda v, j=j: img(v[:, c, :])[:, :, PATCH0[j]:PATCH0[j] + TILE])
                                for j in range(4)]

                    gn(0, inst[which], ACT_BASE[which], SRC[which], free, parts)

                def mask():
                    act.wait_ge(mask_vec, 13)
                    for k in range(2):
                        for c in range(NC):
                            nc.scalar.activation(dist[:, k, c, :], grid[:, :], ACT.Abs,
                                                 bias=cen[:, 4, 2 * k + c:2 * k + c + 1]).then_inc(mask_dist, 1)
                    for c in range(NC):
                        act.wait_ge(mask_vec, 19 + 2 * c)
                        nc.scalar.activation(pad[:, c, 1:HH + 1, 1:WW + 1], img(msk[:, :]), ACT.Relu).then_inc(relu_done, 1)

                def turn_patches(p, c, k):
                    act.wait_ge(turned, 4 * (2 * p + c) + k + 1)
                    if p and k == 0:
                        act.wait_ge(up_sum, N_UP * (2 * p + c - 1))
                    nc.scalar.copy(xt[0:KP, c, 4 * k:4 * k + 4, :],
                                   bank(ring(p, c, k))[0:KP, :].rearrange("p (j n) -> p j n", n=P)).then_inc(turn_copied, 1)

                def up(p, c, u):
                    y = N_UP * (2 * p + c) + u
                    act.wait_ge(up_sum, y + 1)
                    if y >= NY:
                        act.wait_ge(down_sum, y - NY + 1)
                    nc.scalar.activation(ys[0:KP, y % NY, :], bank(ring(p, c, 4 + u))[0:KP, :], ACT.Relu,
                                         scale=1.0 - SLOPE).then_inc(up_relu, 1)

                def b_gn():
                    gn(1, 0, 0, x2, [], lambda c: [(g2[:, c, :], lambda v: v[:, c, :])])

                def b_in(m):
                    act.wait_ge(slot_full, full(("b_in", m)))
                    nc.scalar.activation((xs, zs)[m][:, :].rearrange("p (a b) -> p a b", a=2), slot(("b_in", m))[:, :, 0:HALF],
                                         ACT.Identity, bias=in_b[:, m:m + 1]).then_inc(b_copied, 1)
                    if m == 1:
                        act.wait_ge(gate_z, 1)
                        nc.scalar.activation(sz[:, :], sz[:, :], ACT.Exp, scale=-1.0).then_inc(gate_exp, 1)

                def b_f1():
                    act.wait_ge(slot_full, full(("b_f1", 0)))
                    nc.scalar.activation(f1[:, :].rearrange("p (a b) -> p a b", a=2), slot(("b_f1", 0))[:, :, 0:HALF],
                                         ACT.Identity, bias=c_b[:, 0:1]).then_inc(b_copied, 1)

                def b_f2():
                    act.wait_ge(slot_full, full(("b_f2", 0)))
                    nc.scalar.activation(f2[:, :], slot(("b_f2", 0))[:, 0, 0:LEN[1]], ACT.Identity, bias=c_b[:, 1:2]).then_inc(b_copied, 1)

                def b_f3():
                    act.wait_ge(slot_full, full(("b_f3", 0)))
                    nc.scalar.activation(f3[:, :], slot(("b_f3", 0))[:, 0, 0:LEN[2]], ACT.Identity, bias=c_b[:, 2:3]).then_inc(b_copied, 1)

                def wide(buf, n):
                    return buf[:, 0:n].rearrange("p (a b) -> p a b", a=2) if n == HW else buf[:, 0:n]

                def wide_ps(s, n, p0=0):
                    return s[p0:, :, 0:HALF] if n == HW else s[p0:, 0, 0:n]

                def prep(q):
                    lev, w = BRANCH[q]
                    n = LEN[lev]
                    act.wait_ge(slot_full, full(("V", q)))
                    if q:
                        act.wait_ge(delta_done, q)
                    nc.scalar.activation(wide(va, n), wide_ps(slot(("V", q)), n), ACT.Identity, bias=dt_b[:, w:w + 1]).then_inc(v_act, 1)
                    act.wait_ge(v_act, 4 * q + 1)
                    nc.scalar.activation(vb[:, 0:n], va[:, 0:n], ACT.Abs).then_inc(v_act, 1)
                    act.wait_ge(slot_full, full(("BC", q)))
                    nc.scalar.copy(wide(part(bct, q), n), wide_ps(slot(("BC", q)), n)).then_inc(hi_done, 1)
                    act.wait_ge(v_act, 4 * q + 2)
                    nc.scalar.activation(vb[:, 0:n], vb[:, 0:n], ACT.Exp, scale=-1.0).then_inc(v_act, 1)

                def split(q):
                    n = LEN[BRANCH[q][0]]
                    act.wait_ge(rest_done, q + 1)
                    nc.scalar.copy(part(bct, q)[64:, :], rest[64:, 0:n]).then_inc(mid_done, 1)
                    act.wait_ge(v_act, 4 * q + 3)
                    nc.scalar.activation(vc[:, 0:n], vb[:, 0:n], ACT.Ln, bias=1.0).then_inc(v_act, 1)

                def dbx(k):
                    q, g = SCAN_STEPS[k]
                    lev, w = BRANCH[q]
                    act.wait_ge(delta_done, q + 1)
                    if k == 5:
                        act.wait_ge(slot_full, full(("b_in", 1)))
                    before = [j for j, s in enumerate(SCANS) if (s[0] == k - 2 and lev == 0 and k >= 7) or (s[0] == k - 1 and lev == 1 and g)]
                    if before:
                        act.wait_ge(scan_done, before[-1] + 1)
                    for i in range(PER_STEP[lev]):
                        s = g * PER_STEP[lev] + i
                        out = da_view(k) if lev == 0 else da_view(k)[:, i, 0:LEN[lev]]
                        nc.scalar.activation(out, part(delta, q), ACT.Exp, scale=a_neg[:, w, s:s + 1]).then_inc(da_done, 1)

                def centre(q):
                    n = norm_width(q)
                    act.wait_ge(centred, q + 1)
                    nc.scalar.activation(va[:, 0:n], vb[:, 0:n], ACT.Square).then_inc(squared, 1)

                def var(q):
                    n = norm_width(q)
                    act.wait_ge(slot_full, full(("var", q)))
                    nc.scalar.activation(wide(vc, n), wide_ps(slot(("var", q)), n), ACT.Ln, bias=eps[:, 1:2]).then_inc(ln_rstd, 1)
                    act.wait_ge(ln_rstd, 2 * q + 1)
                    nc.scalar.activation(vc[:, 0:n], vc[:, 0:n], ACT.Exp, scale=-0.5).then_inc(ln_rstd, 1)

                do = {"x_gn": x_gn, "mask": mask, "turn": turn_patches, "up": up, "b_gn": b_gn, "b_in": b_in,
                      "b_f1": b_f1, "b_f2": b_f2, "b_f3": b_f3, "prep": prep, "split": split, "dbx": dbx, "centre": centre, "var": var}
                for kind, *a in order:
                    if kind in do:
                        do[kind](*a)

            @block.gpsimd
            def _(pool):
                def up(p, c, u):
                    y = N_UP * (2 * p + c) + u
                    pool.wait_ge(up_leaky, y + 1)
                    v = ys[0:KP, y % NY, :]
                    nc.gpsimd.tensor_scalar(v, v, CLAMP, -CLAMP, ALU.min, ALU.max).then_inc(up_clipped, 1)

                def keep():
                    if has_last:
                        pool.wait_ge(layer_added, 4)
                    nc.gpsimd.tensor_copy(x3[:, :, :], x2[:, :, :]).then_inc(x2_copied, 1)

                def b_in(m):
                    if m == 1:
                        pool.wait_ge(gate_exp, 1)
                        nc.gpsimd.tensor_scalar(sz[:, :], sz[:, :], 1.0, None, ALU.add).then_inc(gate_fin, 1)

                def b_f2():
                    pool.wait_ge(gate_mul, 1)
                    nc.gpsimd.tensor_tensor(sz[:, :], sz[:, :], zs[:, :], ALU.mult).then_inc(gate_fin, 1)

                def split(q):
                    n = LEN[BRANCH[q][0]]
                    pool.wait_ge(v_act, 4 * q + 3)
                    nc.gpsimd.tensor_scalar(poly[:, 0:n], vb[:, 0:n], 1.0 / 3.0, -0.5, ALU.mult, ALU.add).then_inc(v_pool, 1)
                    nc.gpsimd.tensor_scalar(far[:, 0:n], vb[:, 0:n], SERIES_UNTIL, None, ALU.is_ge).then_inc(v_pool, 1)
                    pool.wait_ge(v_pool, 3 * q + 1)
                    nc.gpsimd.tensor_tensor(poly[:, 0:n], poly[:, 0:n], vb[:, 0:n], ALU.mult).then_inc(v_pool, 1)

                def delta_x(q):
                    lev = BRANCH[q][0]
                    pool.wait_ge(delta_done, q + 1)
                    nc.gpsimd.tensor_tensor(part(dx, q), part(delta, q), F[lev][:, :], ALU.mult).then_inc(dx_done, 1)

                def hc(k):
                    for j in SCANS_OF[k]:
                        if j not in POOL_COUNT:
                            continue
                        _, q, g, d = SCANS[j]
                        lev = BRANCH[q][0]
                        pool.wait_ge(hc_done, j + 1)
                        if POOL_COUNT[j] > 1:
                            pool.wait_ge(state_added, POOL_COUNT[j] - 1)
                        h = h_view(j) if lev == 0 else h_view(j)[:, :, 0:LEN[lev]]
                        a = acc[:, d, :] if lev == 0 else acc[:, d, :].rearrange("p (n l) -> p n l", l=LEN[lev])
                        nc.gpsimd.tensor_tensor(a, a, h, ALU.add).then_inc(state_added, 1)

                do = {"up": up, "keep": keep, "b_in": b_in, "b_f2": b_f2, "split": split, "delta": delta_x, "hc": hc}
                for kind, *a in order:
                    if kind in do:
                        do[kind](*a)

            @block.vector
            def _(dve):
                def gn(x, i, act_base, src):
                    b = 10 * i
                    at = (ps[:, 0, 496:500] if x == 0 else ps[:, 4, 496:500])
                    for c in range(NC):
                        for half in range(2):
                            nc.vector.bn_stats(st[x][:, c, half, :], src[:, c, half * HALF:(half + 1) * HALF]).then_inc(gn_vec[x], 1)
                    dve.wait_ge(gn_vec[x], b + 4)
                    for c in range(NC):
                        nc.vector.bn_aggr(mv[x][:, c, :], st[x][:, c, :, :].rearrange("p a b -> p (a b)")).then_inc(gn_vec[x], 1)
                    dve.wait_ge(gn_mm[x], 2 * i + 1)
                    dve.wait_ge(gn_vec[x], b + 6)
                    nc.vector.tensor_tensor(dev[x][:, 0, :], mv[x][:, :, 0], at[:, 0:2], ALU.subtract).then_inc(gn_vec[x], 1)
                    dve.wait_ge(gn_vec[x], b + 7)
                    nc.vector.tensor_tensor(dev[x][:, 1, :], dev[x][:, 0, :], dev[x][:, 0, :], ALU.mult).then_inc(gn_vec[x], 1)
                    dve.wait_ge(gn_vec[x], b + 8)
                    nc.vector.tensor_tensor(dev[x][:, 2, :], dev[x][:, 1, :], mv[x][:, :, 1], ALU.add).then_inc(gn_vec[x], 1)
                    dve.wait_ge(gn_act[x], act_base + 2)
                    nc.vector.scalar_tensor_tensor(out=nbias[x][:, :], in0=at[:, 0:2], scalar=-1.0, in1=rstd[x][:, :],
                                                   op0=ALU.mult, op1=ALU.mult).then_inc(gn_vec[x], 1)

                def x_gn(which):
                    if which == "conv":
                        dve.wait_ge(x_loaded, 16)
                    if which == "first":
                        dve.wait_ge(conv_added, 4)
                    gn(0, inst[which], ACT_BASE[which], SRC[which])

                def b_gn():
                    gn(1, 0, 0, x2)

                def mask():
                    n = [0]

                    def step(ins):
                        n[0] += 1
                        ins.then_inc(mask_vec, 1)

                    dve.wait_ge(gn_act[0], normed("conv", 1))
                    step(nc.vector.tensor_reduce(lines[:, 0, :, :], xg[:, :, :].rearrange("p c (h w) -> p c h w", w=WW), AX, ALU.add))
                    step(nc.vector.tensor_reduce(lines[:, 1, :, :], xg[:, :, :].rearrange("p c (h w) -> p c w h", w=WW), AX, ALU.add))
                    dve.wait_ge(mask_vec, 2)
                    step(nc.vector.tensor_tensor(wlines[:, :, :, :].rearrange("p a c h -> p (a c) h"),
                                                 lines[:, :, :, :].rearrange("p a c h -> p (a c) h"), ramp[:, :, :], ALU.mult))
                    step(nc.vector.tensor_reduce(s0[:, :, :], lines[:, :, :, :], AX, ALU.add))
                    dve.wait_ge(mask_vec, 4)
                    step(nc.vector.tensor_reduce(s1[:, :, :], wlines[:, :, :, :], AX, ALU.add))
                    step(nc.vector.tensor_scalar(cen[:, 0, 0:2], s0[:, 0, :], 1e-9, None, ALU.max))
                    dve.wait_ge(mask_vec, 6)
                    step(nc.vector.reciprocal(cen[:, 0, 2:4], cen[:, 0, 0:2]))
                    dve.wait_ge(mask_vec, 7)
                    step(nc.vector.tensor_tensor(cen[:, 1, 0:2], s1[:, 0, :], cen[:, 0, 2:4], ALU.mult))
                    step(nc.vector.tensor_tensor(cen[:, 1, 2:4], s1[:, 1, :], cen[:, 0, 2:4], ALU.mult))
                    dve.wait_ge(mask_vec, 9)
                    step(nc.vector.tensor_scalar(cen[:, 2, :], cen[:, 1, :], 1.0, float(HH), ALU.max, ALU.min))
                    dve.wait_ge(mask_vec, 10)
                    step(nc.vector.tensor_scalar(cen[:, 3, :], cen[:, 2, :], MAGIC, None, ALU.add))
                    dve.wait_ge(mask_vec, 11)
                    step(nc.vector.tensor_scalar(cen[:, 2, :], cen[:, 3, :], MAGIC, None, ALU.subtract))
                    dve.wait_ge(mask_vec, 12)
                    step(nc.vector.tensor_scalar(cen[:, 4, :], cen[:, 2, :], 1.0, -STEP, ALU.subtract, ALU.mult))
                    for k in range(2):
                        for c in range(NC):
                            dve.wait_ge(mask_dist, 2 * k + c + 1)
                            step(nc.vector.tensor_scalar(ahbw[:, k, c, :], dist[:, k, c, :], neg_mw[:, c:c + 1],
                                                         1.0 - k, ALU.mult, ALU.add))
                    for c in range(NC):
                        if c:
                            dve.wait_ge(relu_done, 1)
                        dve.wait_ge(mask_vec, 17 + 2 * c)
                        step(nc.vector.tensor_tensor(img(msk[:, :]), ahbw[:, 0, c, :].unsqueeze(2).broadcast_to([P, HH, WW]),
                                                     ahbw[:, 1, c, :].unsqueeze(1).broadcast_to([P, HH, WW]), ALU.add))
                        dve.wait_ge(mask_vec, 18 + 2 * c)
                        step(nc.vector.scalar_tensor_tensor(out=msk[:, :], in0=msk[:, :], scalar=-1.0, in1=xg[:, c, :],
                                                            op0=ALU.max, op1=ALU.mult))

                def conv(g):
                    m, half = divmod(g, 2)
                    dve.wait_ge(conv_sum, g + 1)
                    v = xa[:, m, half * HALF:(half + 1) * HALF]
                    nc.vector.scalar_tensor_tensor(out=v, in0=ps[:, half, 0:HALF], scalar=conv_b[:, m:m + 1], in1=v,
                                                   op0=ALU.add, op1=ALU.add).then_inc(conv_added, 1)

                def up(p, c, u):
                    y = N_UP * (2 * p + c) + u
                    dve.wait_ge(up_relu, y + 1)
                    v = ys[0:KP, y % NY, :]
                    nc.vector.scalar_tensor_tensor(out=v, in0=bank(ring(p, c, 4 + u))[0:KP, :], scalar=SLOPE, in1=v,
                                                   op0=ALU.mult, op1=ALU.add).then_inc(up_leaky, 1)

                def fin(p, c):
                    which = passes[p]
                    dve.wait_ge(down_sum, N_UP * (2 * p + c + 1))
                    src, dst = SRC[which], (xg if which == "last" else x2)
                    if which == "first" and has_b:
                        dve.wait_ge(gn_act[1], 4)
                        dve.wait_ge(x2_copied, 1)
                    for reg in range(2):
                        a, b = ((0, SPLIT * WW), (SPLIT * WW, HW))[reg]
                        nc.vector.tensor_tensor(dst[:, c, a:b], src[:, c, a:b], ps[:, reg, 0:b - a], ALU.add).then_inc(layer_added, 1)

                def b_in(m):
                    if m == 1:
                        dve.wait_ge(b_copied, 2)
                        nc.vector.tensor_scalar(sz[:, :], zs[:, :], -80.0, None, ALU.max).then_inc(gate_z, 1)

                def b_f1():
                    dve.wait_ge(gate_fin, 1)
                    nc.vector.reciprocal(sz[:, :], sz[:, :]).then_inc(gate_mul, 1)

                def split(q):
                    lev, w = BRANCH[q]
                    n = LEN[lev]
                    dve.wait_ge(hi_done, q + 1)
                    if q:
                        dve.wait_ge(bct_done, q)
                    s = slot(("BC", q))
                    if n == HW:
                        nc.vector.tensor_tensor(rest[64:, :].rearrange("p (a b) -> p a b", a=2), s[64:, :, 0:HALF],
                                                part(bct, q)[64:, :].rearrange("p (a b) -> p a b", a=2), ALU.subtract).then_inc(rest_done, 1)
                    else:
                        nc.vector.tensor_tensor(rest[64:, 0:n], s[64:, 0, 0:n], part(bct, q)[64:, :], ALU.subtract).then_inc(rest_done, 1)

                def delta_of(q):
                    n = LEN[BRANCH[q][0]]
                    dve.wait_ge(v_pool, 3 * q + 3)
                    nc.vector.scalar_tensor_tensor(out=poly[:, 0:n], in0=poly[:, 0:n], scalar=1.0, in1=vb[:, 0:n],
                                                   op0=ALU.add, op1=ALU.mult).then_inc(v_series, 1)
                    dve.wait_ge(v_series, q + 1)
                    dve.wait_ge(v_act, 4 * q + 4)
                    nc.vector.copy_predicated(poly[:, 0:n], far[:, 0:n].bitcast(mybir.dt.uint32), vc[:, 0:n]).then_inc(v_log, 1)
                    dve.wait_ge(v_log, q + 1)
                    nc.vector.scalar_tensor_tensor(out=part(delta, q), in0=va[:, 0:n], scalar=0.0, in1=poly[:, 0:n],
                                                   op0=ALU.max, op1=ALU.add).then_inc(delta_done, 1)
                    dve.wait_ge(mid_done, q + 1)
                    nc.vector.tensor_tensor(part(bct, q)[96:, :], rest[96:, 0:n], part(bct, q)[96:, :], ALU.subtract).then_inc(bct_done, 1)

                def dbx(k):
                    q, g = SCAN_STEPS[k]
                    lev, w = BRANCH[q]
                    dve.wait_ge(slot_full, full(("B", k)))
                    dve.wait_ge(dx_done, q + 1)
                    if k == 5:
                        dve.wait_ge(delta_done, 4)
                    s = slot(("B", k))[:, :, 0:HALF]
                    if lev == 0:
                        nc.vector.tensor_tensor(db_view(k).rearrange("p (a b) -> p a b", a=2), s,
                                                part(dx, q).rearrange("p (a b) -> p a b", a=2), ALU.mult).then_inc(dbx_done, 1)
                    else:
                        n, per = LEN[lev], PER_STEP[lev] // 2
                        if lev == 1 and g:
                            dve.wait_ge(scan_done, LAST_SCAN[k - 1] + 1)
                        nc.vector.tensor_tensor(db_view(k)[:, :, 0:n].rearrange("p (a b) l -> p a b l", a=2),
                                                s.rearrange("p a (b l) -> p a b l", l=n),
                                                part(dx, q).unsqueeze(1).unsqueeze(1).broadcast_to([P, 2, per, n]),
                                                ALU.mult).then_inc(dbx_done, 1)

                def scan(k):
                    q, g = SCAN_STEPS[k]
                    lev = BRANCH[q][0]
                    done = sum(PER_STEP[BRANCH[SCAN_STEPS[i][0]][0]] for i in range(k + 1))
                    dve.wait_ge(da_done, done)
                    dve.wait_ge(dbx_done, k + 1)
                    for j in SCANS_OF[k]:
                        d = SCANS[j][3]
                        last = j - NH
                        if last in (0, 1):
                            dve.wait_ge(fold_done, 2)
                        elif last in POOL_COUNT:
                            dve.wait_ge(state_added, POOL_COUNT[last])
                        elif last >= 0:
                            dve.wait_ge(hc_done, last + 1)
                        n = HW if lev == 0 else PER_STEP[lev] * (LEN[lev] + 1)
                        a, b = [v if lev == 0 else v[:, :, :].rearrange("p n l -> p (n l)") for v in (da_view(k), db_view(k))]
                        h = hs[:, j % NH, 0:n]
                        if d:
                            a, b, h = a[:, ::-1], b[:, ::-1], h[:, ::-1]
                        nc.vector.tensor_tensor_scan(h, a, b, 0.0, ALU.mult, ALU.add).then_inc(scan_done, 1)

                def hc(k):
                    q, g = SCAN_STEPS[k]
                    lev = BRANCH[q][0]
                    dve.wait_ge(slot_full, full(("C", k)))
                    s = slot(("C", k))[:, :, 0:HALF]
                    for j in SCANS_OF[k]:
                        d = SCANS[j][3]
                        dve.wait_ge(scan_done, j + 1)
                        h = h_view(j)
                        if lev == 0:
                            h3 = h.rearrange("p (a b) -> p a b", a=2)
                            o = acc[:, d, :].rearrange("p (a b) -> p a b", a=2) if g == 0 else h3
                            if g == 0:
                                dve.wait_ge(fold_done, 4)
                        else:
                            n = LEN[lev]
                            h3 = h[:, :, 0:n].rearrange("p (a b) l -> p a b l", a=2)
                            s = slot(("C", k))[:, :, 0:HALF].rearrange("p a (b l) -> p a b l", l=n)
                            o = acc[:, d, :].rearrange("p (a b l) -> p a b l", a=2, l=n) if g == 0 and lev == 1 else h3
                        nc.vector.tensor_tensor(o, s, h3, ALU.mult).then_inc(hc_done, 1)

                def fold(q):
                    n = LEN[BRANCH[q][0]]
                    if q == 1:
                        dve.wait_ge(state_added, POOL_COUNT[max(j for j, s in enumerate(SCANS) if s[1] == 1)])
                        dve.wait_ge(bct_done, 4)
                    else:
                        dve.wait_ge(hc_done, 2)
                    for d in range(2):
                        src = (acc[:, d, :].rearrange("p (n l) -> p l n", l=n) if q == 1 else
                               h_view(d)[:, :, 0:n].rearrange("p n l -> p l n"))
                        nc.vector.tensor_reduce((sums3, rest)[q][:, d * n:(d + 1) * n], src, AX, ALU.add).then_inc(fold_done, 1)

                def y_of(q):
                    lev, w = BRANCH[q]
                    n = LEN[lev]
                    if q == 0:
                        dve.wait_ge(delta_done, 4)
                        dve.wait_ge(v_act, 16)
                    else:
                        dve.wait_ge(slot_full, full(("var", q - 1)))
                    if lev == 0:
                        dve.wait_ge(state_added, POOL_COUNT[max(j for j, s in enumerate(SCANS) if s[1] == q)])
                    else:
                        dve.wait_ge(fold_done, 2 * q + 2)
                    for d in range(2 if lev else 1):
                        src = acc[:, q - 2, :] if lev == 0 else (sums3, rest)[q][:, d * n:(d + 1) * n]
                        ins = nc.vector.scalar_tensor_tensor(out=va[:, d * n:(d + 1) * n], in0=F[lev][:, :], scalar=dv[:, w:w + 1],
                                                             in1=src, op0=ALU.mult, op1=ALU.add)
                    ins.then_inc(y_done, 1)

                def centre(q):
                    width = norm_width(q)
                    dve.wait_ge(slot_full, full(("mean", q)))
                    dve.wait_ge(y_done, q + 1)
                    if q:
                        dve.wait_ge(y_mixed, mixed_until(q))
                    s = slot(("mean", q))
                    if width == HW:
                        nc.vector.tensor_tensor(vb[:, :].rearrange("p (a b) -> p a b", a=2), va[:, :].rearrange("p (a b) -> p a b", a=2),
                                                s[:, :, 0:HALF], ALU.subtract).then_inc(centred, 1)
                    else:
                        nc.vector.tensor_tensor(vb[:, 0:width], va[:, 0:width], s[:, 0, 0:width], ALU.subtract).then_inc(centred, 1)

                def mix(q):
                    lev, w = BRANCH[q]
                    n, width = LEN[lev], norm_width(q)
                    dve.wait_ge(ln_rstd, 2 * q + 2)
                    dve.wait_ge(centred, q + 1)
                    g = ln_g[:, w:w + 1]
                    m = mixed_until(q)
                    if q == 3:
                        nc.vector.scalar_tensor_tensor(out=vb[:, :], in0=vb[:, :], scalar=g, in1=vc[:, :], op0=ALU.mult, op1=ALU.mult).then_inc(y_mixed, 1)
                        dve.wait_ge(y_mixed, m + 1)
                        nc.vector.tensor_tensor(y1[:, :], y1[:, :], vb[:, :], ALU.add).then_inc(y_mixed, 1)
                        return
                    if q == 2:
                        nc.vector.scalar_tensor_tensor(out=y1[:, :], in0=vb[:, :], scalar=g, in1=vc[:, :], op0=ALU.mult, op1=ALU.mult).then_inc(y_mixed, 1)
                        fine, coarse, side = y1, y2, HH
                    else:
                        nc.vector.scalar_tensor_tensor(out=vb[:, 0:width], in0=vb[:, 0:width], scalar=g, in1=vc[:, 0:width],
                                                       op0=ALU.mult, op1=ALU.mult).then_inc(y_normed, 1)
                        dve.wait_ge(y_normed, q + 1)
                        fine, coarse, side = (y3, None, 0) if q == 0 else (y2, y3, HH // 2)
                        nc.vector.tensor_tensor(fine[:, :], vb[:, 0:n], vb[:, n:2 * n], ALU.add).then_inc(y_mixed, 1)
                    if coarse is not None:
                        dve.wait_ge(y_mixed, m + 1)
                        for r in range(2):
                            o = img(fine[:, :], side)[:, r:side:2, :].rearrange("p h (w s) -> p h w s", s=2)
                            nc.vector.tensor_tensor(o, o, img(coarse[:, :], side // 2).unsqueeze(3).broadcast_to([P, side // 2, side // 2, 2]),
                                                    ALU.add).then_inc(y_mixed, 1)

                def gate():
                    dve.wait_ge(y_mixed, mixed_until(4))
                    dve.wait_ge(gate_fin, 2)
                    nc.vector.scalar_tensor_tensor(out=y1[:, :], in0=y1[:, :], scalar=bias_sum[:, 0:1], in1=sz[:, :],
                                                   op0=ALU.add, op1=ALU.mult).then_inc(gated, 1)

                def b_out(m):
                    dve.wait_ge(slot_full, full(("b_out", m)))
                    dve.wait_ge(x2_copied, 1)
                    v = x3[:, m, :].rearrange("p (a b) -> p a b", a=2)
                    nc.vector.scalar_tensor_tensor(out=v, in0=slot(("b_out", m))[:, :, 0:HALF], scalar=out_b[:, m:m + 1], in1=v,
                                                   op0=ALU.add, op1=ALU.add).then_inc(x3_done, 1)

                do = {"x_gn": x_gn, "mask": mask, "conv": conv, "up": up, "fin": fin, "b_gn": b_gn, "b_in": b_in, "b_f1": b_f1,
                      "split": split, "delta": delta_of, "dbx": dbx, "scan": scan, "hc": hc, "fold": fold, "y": y_of, "centre": centre,
                      "mix": mix, "gate": gate, "b_out": b_out}
                for kind, *a in order:
                    if kind in do:
                        do[kind](*a)

        def sample(arr, i):
            return arr[bass.ds(i, 1)].rearrange("o (c p) h w -> p (o c) (h w)", p=P)

        def between():
            ids = [s.num for s in turn_sems]
            nc.gpsimd.sem_clear(range(min(ids), max(ids) + 1))
            nc.all_engine_barrier()

        def run(i, has_b, has_last, has_first):
            with nc.Block() as block:
                turn(block, has_b, has_last, has_first,
                     sample(t["x"], i + 1) if has_first else None, sample(t["out"], i - 1) if has_last else None)
            between()

        run(-1, False, False, True)
        run(0, True, False, True)
        with nc.Fori(1, N_SAMPLES - 1) as i:
            run(i, True, True, True)
        run(N_SAMPLES - 1, True, True, False)
        run(N_SAMPLES, False, True, False)


def lay_out(inputs):
    import numpy as np
    g = {k: np.asarray(v) for k, v in inputs.items()}

    def cols(v):
        return np.ascontiguousarray(v.reshape(-1, P).T)

    L2 = {k[len("L2_conv_"):]: v for k, v in g.items() if k.startswith("L2_conv_")}
    a = {"x": g["x"]}
    a["conv_w"] = g["L0_conv_weight"].reshape(CH, NC, P, 9).transpose(2, 1, 3, 0)
    a["conv_b"] = cols(g["L0_conv_bias"])
    a["mask_w"] = cols(g["L0_conv_mask_weight"])
    a["filt"] = cols(g["L0_conv_filter"].reshape(-1))
    a["in_w"] = L2["in_w"].reshape(CH, NC, P).transpose(2, 1, 0)
    a["in_b"] = cols(L2["in_b"])
    a["c1_w"] = L2["c1_w"].T
    a["c23_w"] = np.stack([L2["c2_w"], L2["c3_w"]]).reshape(2, P, P, 4).transpose(2, 0, 3, 1)
    a["c_b"] = np.stack([L2["c1_b"], L2["c2_b"], L2["c3_b"]], 1)
    a["out_w"] = L2["out_w"].T
    a["out_b"] = cols(L2["out_b"])
    xw = np.stack([L2[f"xw{i}"] for i in (1, 2, 3)])
    dtw = np.stack([L2[f"dtw{i}"] for i in (1, 2, 3)])
    bc = xw[:, R_DT:, :].transpose(2, 0, 1)
    a["bc_w"] = np.repeat(bc[:, :, None, :], 4, axis=2)
    a["dt_parts"] = np.stack([xw[:, :R_DT, :].transpose(1, 0, 2), dtw.transpose(2, 0, 1)], 2).reshape(R_DT, 6 * P)
    for name, key in (("dt_b", "dtb"), ("dv", "Dv"), ("ln_g", "g"), ("ln_b", "be")):
        a[name] = np.stack([L2[f"{key}{i}"] for i in (1, 2, 3)], 1)
    a["al"] = np.stack([L2[f"Al{i}"] for i in (1, 2, 3)], 1)
    taps = np.zeros((4, 2, KP, 4, KP), np.float32)
    i, j = np.divmod(np.arange(KP), TILE)
    for n in range(4):
        f = g[f"L{1 + 2 * (n // 2)}_conv_{'down' if n % 2 else 'up'}_filter"][::-1]
        line = np.concatenate([np.zeros(64, f.dtype), f, np.zeros(64, f.dtype)])
        for side, r in enumerate((i, j)):
            for k in range(4):
                if n % 2 == 0:
                    at = 2 * r[:, None] - r[None, :] + (11, 0, 1, -10)[k]
                else:
                    at = r[:, None] - 2 * r[None, :] + (0, 11, 10, 21)[k]
                taps[n, side, :, k, :] = line[at + 64]
    a["taps"] = taps.reshape(4, 2, KP, 4 * KP)
    b = np.stack([g["L1_conv_bias"], g["L3_conv_bias"]]).reshape(2, NC, 1, P)
    a["bias_rows"] = np.repeat(b, 16, axis=2)
    on = np.zeros((2, 2, 16, KP), np.float32)
    on[0, 0] = on[1, 1] = SQRT2
    a["bias_on"] = on
    n = np.arange(P)
    a["ident"] = np.eye(P, dtype=np.float32)
    a["group_mean"] = (n[:, None] // GROUP == n[None, :] // GROUP).astype(np.float32) / np.float32(GROUP)
    a["chan_mean"] = np.full((P, P), 1.0 / P, np.float32)
    pick = np.zeros((P, 2 * N_STATE), np.float32)
    for base in (0, 64, 96):
        pick[base:base + 32] = np.eye(32, dtype=np.float32)
    a["pick"] = pick
    a["ramp"] = np.tile(np.arange(1, HH + 1, dtype=np.float32), (P, 4, 1))
    a["grid"] = np.tile((np.arange(HH) * STEP).astype(np.float32), (P, 1))
    return {k: np.ascontiguousarray(v) for k, v in a.items()}


def kernel(**inputs):
    import concourse.bacc as _bacc
    from concourse.bass_utils import run_bass_kernel_spmd as _run

    nc = _bacc.Bacc("TRN2", target_bir_lowering=False, num_devices=1)
    arrays = lay_out(inputs)
    t = {k: nc.dram_tensor(f"in_{k}", v.shape, mybir.dt.from_np(v.dtype), kind="ExternalInput").ap() for k, v in arrays.items()}
    t["out"] = nc.dram_tensor("out_0", arrays["x"].shape, F32, kind="ExternalOutput").ap()
    build(nc, t)
    r = _run(nc, [{f"in_{k}": v for k, v in arrays.items()}], core_ids=[0])
    return r.results[0]["out_0"]
```

```python
from contextlib import ExitStack

import concourse.bass as bass
from concourse import mybir

F32 = mybir.dt.float32
BF16 = mybir.dt.bfloat16
ALU = mybir.AluOpType
ACT = mybir.ActivationFunctionType
AX = mybir.AxisListType.X

P = 128
N_SAMPLES, CH, HH, WW = 32, 256, 28, 28
HW = HH * WW
NC = CH // P
HALF = HW // 2
GROUP = 8
GN_EPS = 1e-5
LN_EPS = 1e-5
MAGIC = 12582912.0
SERIES_UNTIL = 2.0 ** -6
STEP = 2.0 / (HH - 1)

TILE = 11
KP = TILE * TILE
TAPS = 9
PATCH0 = [0, 6, 11, 17]
TYPE_TILES = [[0], [1, 3], [2, 4], [5]]
TYPE_PATCHES = [[0], [0, 2], [1, 3], [3]]
TILE_PATCH = [0, 0, 1, 2, 3, 3]
TILE_ROWS = [(0, 6), (0, 11), (0, 11), (0, 11), (0, 11), (5, 11)]
SPLIT = 17
UP_STEPS = ([[(a, b)] for a in (1, 2) for b in (1, 2)]
            + [[(a, 1), (a, 2)] for a in (0, 3)] + [[(1, b), (2, b)] for b in (0, 3)]
            + [[(0, 0), (0, 3), (3, 0), (3, 3)]])
N_UP = len(UP_STEPS)
CLAMP = 256.0
SLOPE = 0.2
UP_GAIN = SLOPE * 2.0 ** 0.5

N_STATE = 16
R_DT = 8
LEN = [HW, HW // 4, HW // 16]
BRANCH = [(2, 2), (1, 1), (0, 0), (0, 1)]
PER_STEP = [1, 4, 16]
SCAN_STEPS = [(q, g) for q, (lev, _) in enumerate(BRANCH) for g in range(N_STATE // PER_STEP[lev])]
SCANS = [(k, q, g, d) for k, (q, g) in enumerate(SCAN_STEPS)
         for d in ((0, 1) if BRANCH[q][0] else ((0,) if q == 2 else (1,)))]
POOL_ADDS = [j for j, (k, q, g, d) in enumerate(SCANS) if g > 0]
LAST_SCAN = {k: j for j, (k, q, g, d) in enumerate(SCANS)}
SCANS_OF = {k: [j for j, s in enumerate(SCANS) if s[0] == k] for k in range(len(SCAN_STEPS))}


B_SEQUENCE = [0, 1, 2, 3, 4, 5, 6, 8, 10, 12, 13, 14, 15, 24, 25, 29, 17, 18, 27, 37, 16, 41, 20, 26, 19, 21, 46, 23,
            28, 54, 31, 32, 33, 34, 30, 7, 36, 38, 43, 39, 42, 40, 44, 47, 45, 48, 51, 52, 56, 9, 50, 49, 70, 35, 58,
            66, 64, 74, 79, 53, 59, 57, 65, 55, 61, 77, 83, 84, 75, 60, 69, 76, 86, 62, 85, 78, 63, 71, 67, 72, 91,
            73, 81, 80, 90, 87, 92, 103, 95, 89, 98, 97, 93, 99, 101, 102, 96, 106, 111, 110, 104, 82, 113, 94, 105,
            108, 116, 118, 107, 100, 112, 114, 119, 115, 117, 125, 124, 131, 121, 109, 126, 129, 133, 123, 130, 132,
            68, 137, 138, 120, 139, 11, 136, 127, 128, 145, 134, 141, 135, 88, 140, 152, 143, 147, 154, 159, 146, 150,
            153, 144, 142, 148, 151, 149, 158, 161, 157, 155, 156, 162, 163, 160, 164, 165, 168, 169, 166, 167, 174,
            173, 180, 175, 171, 178, 170, 176, 181, 172, 182, 185, 189, 187, 188, 177, 199, 179, 183, 190, 186, 200,
            198, 184, 192, 207, 201, 209, 194, 208, 210, 195, 196, 191, 212, 214, 213, 204, 215, 203, 211, 205, 216,
            222, 217, 221, 225, 220, 223, 224, 219, 226, 230, 228, 227, 122, 229, 231, 193, 236, 234, 235, 232, 239,
            242, 233, 197, 240, 237, 202, 244, 241, 243, 250, 248, 246, 238, 245, 251, 247, 249, 253, 258, 254, 257,
            256, 255, 252, 259, 260, 264, 263, 267, 265, 262, 269, 261, 270, 271, 274, 266, 22, 277, 268, 275, 272,
            273, 279, 278, 281, 276, 280, 282, 284, 286, 285, 288, 292, 206, 291, 293, 295, 283, 290, 287, 294, 297,
            289, 298, 218, 296, 299, 300, 301, 302, 303, 304, 305, 306]


def scan_layer_order():
    order = [("b_gn", 0), ("b_gn", 1), ("b_gn", 2), ("b_gn", 3), ("b_f1",), ("b_f2",), ("b_f3",), ("b_in",),
             ("prep", 0), ("gate_z",), ("split", 0), ("gate_exp",), ("delta", 0),
             ("prep", 1), ("split", 1), ("delta", 1), ("cast_b", 0), ("decay", 0), ("dbx", 0)]
    between = {1: [("split", 2)], 2: [("delta", 2)], 3: [("split", 3)], 4: [("delta", 3)],
               5: [("fold", 1)], 6: [("y", 0)], 7: [("centre", 0)], 8: [("gate_mul",)], 9: [("mix", 0), ("y", 1)], 10: [("centre", 1)],
               12: [("mix", 1)], 22: [("y", 2)], 23: [("centre", 2)], 25: [("mix", 2)]}
    ahead = {0: [("fold", 0), ("prep", 2)], 2: [("prep", 3)], 6: [("mean", 0)], 7: [("var", 0)], 9: [("mean", 1)],
             10: [("var", 1)], 22: [("mean", 2)], 23: [("var", 2)]}
    for k in range(len(SCAN_STEPS)):
        following = [("cast_b", k + 1), ("decay", k + 1), ("dbx", k + 1)] if k + 1 < len(SCAN_STEPS) else []
        order += [("scan", k)] + between.get(k, []) + [("cast_c", k)]
        if k in ahead:
            order += [("hc", k), ("add", k)] + ahead[k] + following
        else:
            order += following + [("hc", k), ("add", k)]
    order += [("y", 3), ("mean", 3), ("centre", 3), ("var", 3), ("mix", 3), ("gate",), ("b_out", 0), ("b_out", 1)]
    return order


def slot_uses(order):
    names = []
    for kind, *a in order:
        if kind == "b_out":
            names.append((kind, a[0]))
        elif kind in ("b_in", "b_f1", "b_f2", "b_f3"):
            names.append((kind, 0))
        elif kind == "prep":
            names += [("V", a[0]), ("BC", a[0])]
        elif kind == "cast_b":
            names.append(("B", a[0]))
        elif kind == "cast_c":
            names.append(("C", a[0]))
        elif kind in ("mean", "var"):
            names.append((kind, a[0]))
    return {n: i for i, n in enumerate(names)}


LAST, FIRST = 0, 1


def filter_order(p):
    out = []
    for c in range(NC):
        out += [("turn", p, c, k) for k in range(4)]
        for u in range(N_UP + 2):
            if u < N_UP:
                out.append(("up", p, c, u))
            if 1 <= u <= N_UP:
                out.append(("clip", p, c, u - 1))
            if u >= 2:
                out.append(("down", p, c, u - 2))
        out.append(("fin", p, c))
    return out


X_SEQUENCE = [0, 1, 2, 3, 9, 4, 10, 5, 6, 7, 8, 11, 13, 14, 15, 16, 17, 18, 20, 19, 21, 23, 24, 22, 26, 12, 27, 25, 30,
            28, 29, 31, 32, 35, 34, 33, 38, 36, 37, 39, 45, 46, 47, 41, 40, 42, 48, 49, 50, 43, 44, 51, 52, 53, 55,
            56, 54, 58, 59, 57, 61, 60, 62, 64, 63, 67, 66, 70, 65, 68, 69, 71, 72, 74, 73, 75, 76, 78, 88, 89, 90,
            91, 79, 80, 92, 93, 81, 82, 83, 94, 84, 85, 86, 95, 87, 96, 97, 98, 99, 100, 108, 109, 110, 101, 102, 111,
            112, 113, 114, 103, 104, 115, 105, 106, 116, 107, 117, 118, 77, 119, 120, 122, 123, 124, 125, 126, 128,
            127, 130, 129, 131, 132, 133, 121, 134, 135, 138, 136, 139, 137, 141, 140, 142, 145, 144, 148, 143, 147,
            146, 154, 149, 155, 156, 157, 151, 158, 159, 150, 160, 152, 161, 164, 162, 153, 165, 168, 163, 167, 166,
            170, 171, 174, 169, 173, 172, 176, 175, 177, 179, 178, 180, 182, 181, 183, 184, 185]
B_BEFORE = [5, 5, 5, 5, 8, 8, 11, 12, 13, 14, 19, 19, 22, 23, 26, 26, 28, 29, 29, 33, 34, 34, 36, 36, 37, 39, 39, 39,
            43, 43, 45, 45, 45, 45, 53, 53, 55, 55, 55, 59, 60, 64, 64, 64, 64, 64, 65, 70, 73, 73, 73, 73, 75, 75,
            79, 79, 80, 83, 83, 83, 85, 85, 86, 86, 86, 91, 92, 93, 93, 93, 98, 99, 99, 99, 102, 102, 104, 110, 110,
            114, 117, 119, 127, 128, 134, 135, 141, 141, 145, 150, 150, 152, 155, 167, 167, 169, 174, 176, 178, 178,
            179, 186, 186, 193, 194, 202, 207, 210, 216, 222, 222, 232, 233, 233, 233, 233, 235, 235, 235, 235, 237,
            247, 249, 249, 252, 257, 259, 260, 262, 267, 269, 270, 272, 274, 274, 275, 275, 276, 277, 284, 284, 285,
            285, 287, 293, 296, 296, 297, 297, 297, 297, 299, 299, 299, 299, 300, 300, 301, 302, 302, 302, 302, 302,
            302, 302, 304, 304, 304, 304, 304, 304, 304, 304, 304, 305, 305, 305, 305, 305, 306, 306, 306, 307, 307,
            307, 307]


def full_turn_order():
    b = scan_layer_order()
    x = [("x_gn", "conv", n) for n in range(4)] + [("mask", n) for n in range(5)]
    x += [("x_gn", "last", n) for n in range(4)] + filter_order(LAST) + [("keep",)]
    x += [("conv", g, n) for g in range(4) for n in range(TAPS + 1)]
    x += [("x_gn", "first", n) for n in range(4)] + filter_order(FIRST)
    out, i = [], 0
    for before, j in zip(B_BEFORE, X_SEQUENCE, strict=True):
        out += [b[k] for k in B_SEQUENCE[i:before]] + [x[j]]
        i = max(i, before)
    return out + [b[k] for k in B_SEQUENCE[i:]]


def turn_order(has_b, has_last, has_first):
    out = []
    for kind, *a in full_turn_order():
        if kind in ("mask", "conv") or a[:1] in (["conv"], ["first"]):
            wanted = has_first
        elif a[:1] == ["last"]:
            wanted = has_last
        elif kind in ("turn", "up", "clip", "down", "fin"):
            wanted = (has_last, has_first)[a[0]]
            a = [a[0] if has_last else 0] + a[1:]
        else:
            wanted = has_b
        if wanted:
            out.append((kind, *a))
    return out


def build(nc, t):
    ctx = ExitStack()
    with ctx:
        def sb(name, shape, dt=F32):
            return ctx.enter_context(nc.sbuf_tensor(name, shape, dt))

        SEMS = []

        def sem(name):
            s = ctx.enter_context(nc.semaphore(name))
            SEMS.append(s)
            return s

        ident = sb("ident", [P, P])
        group_mean = sb("group_mean", [P, P])
        chan_mean = sb("chan_mean", [P, P])
        pick = sb("pick", [P, 2 * N_STATE])
        pick_bf = sb("pick_bf", [P, 2 * N_STATE], BF16)
        ramp = sb("ramp", [P, 4, HH])
        grid = sb("grid", [P, HH])
        conv_w = sb("conv_w", [P, NC, 9, CH])
        conv_b = sb("conv_b", [P, NC])
        neg_mw = sb("neg_mw", [P, NC])
        filt = sb("filt", [P, NC])
        up_k = [sb(f"up_k{l}", [P, 16, KP]) for l in range(2)]
        down_k = [sb(f"down_k{l}", [P, 16, TILE, TILE]) for l in range(2)]
        in_w = sb("in_w", [P, NC, CH])
        in_b = sb("in_b", [P, 2])
        c23_w = sb("c23_w", [P, 2, 4, P])
        c_b = sb("c_b", [P, 3])
        out_w = sb("out_w", [P, CH])
        out_b = sb("out_b", [P, NC])
        bc_w = sb("bc_w", [P, 3, 4, 2 * N_STATE])
        dt_w = sb("dt_w", [P, 3, P])
        dt_b = sb("dt_b", [P, 3])
        a_neg = sb("a_neg", [P, 3, N_STATE])
        dv = sb("dv", [P, 3])
        ln_g = sb("ln_g", [P, 3])
        ln_b = sb("ln_b", [P, 3])
        bias_sum = sb("bias_sum", [P, 1])
        eps = sb("eps", [P, 2])

        xa = sb("xa", [P, NC, HW])
        xp = sb("xp", [P, NC, 4, HH * TILE])
        xg = xp[:, :, :, :].rearrange("p c j n -> p c (j n)")[:, :, 0:HW]
        x2 = sb("x2", [P, NC, HW])
        x3 = sb("x3", [P, NC, HW])
        pad = sb("pad", [P, NC, HH + 2, WW + 2])
        msk = sb("msk", [P, HW])
        xt = sb("xt", [P, NC, 16, P])
        NY = 4
        ys = sb("ys", [P, NY, 4 * P])
        d_a0 = sb("d_a0", [P, 2, HW])
        d_b0 = sb("d_b0", [P, 2, HW])
        d_a1 = sb("d_a1", [P, 4, LEN[1] + 1])
        d_b1 = sb("d_b1", [P, 4, LEN[1] + 1])
        d_a2 = sb("d_a2", [P, 16, LEN[2] + 1])
        d_b2 = sb("d_b2", [P, 16, LEN[2] + 1])
        NH = 3
        hs = sb("hs", [P, NH, 16 * (LEN[2] + 1)])
        acc = sb("acc", [P, 2, HW])
        f1 = sb("f1", [P, HW])
        f2 = sb("f2", [P, LEN[1]])
        f3 = sb("f3", [P, LEN[2]])
        zs = sb("zs", [P, HW])
        sz = sb("sz", [P, HW])
        delta = sb("delta", [P, sum(LEN) + HW])
        dx = sb("dx", [P, sum(LEN) + HW])
        bct = sb("bct", [P, sum(LEN) + HW], BF16)
        va = sb("va", [P, HW])
        vb = sb("vb", [P, HW])
        vc = sb("vc", [P, HW])
        y1 = sb("y1", [P, HW])
        y2 = sb("y2", [P, LEN[1]])
        y3 = sb("y3", [P, LEN[2]])
        sums3 = sb("sums3", [P, 2 * LEN[2]])
        g2 = d_a0
        y_sloped = msk[:, 0:4 * P]
        poly, far = d_b0[:, 0, :], d_b0[:, 1, :]
        rest = y1
        st = [sb(f"st{i}", [P, NC, 2, 6]) for i in range(2)]
        mv = [sb(f"mv{i}", [P, NC, 2]) for i in range(2)]
        dev = [sb(f"dev{i}", [P, 3, NC]) for i in range(2)]
        rstd = [sb(f"rstd{i}", [P, NC]) for i in range(2)]
        lnv = [sb(f"lnv{i}", [P, NC]) for i in range(2)]
        nbias = [sb(f"nbias{i}", [P, NC]) for i in range(2)]
        lines = sb("lines", [P, 2, NC, HH])
        wlines = sb("wlines", [P, 2, NC, HH])
        s0 = sb("s0", [P, 2, NC])
        s1 = sb("s1", [P, 2, NC])
        cen = sb("cen", [P, 5, 2 * NC])
        dist = sb("dist", [P, 2, NC, HH])
        ahbw = sb("ahbw", [P, 2, NC, HH])

        ps = ctx.enter_context(nc.psum_tensor("ps", [P, 8, 512], F32))

        F = [f1, f2, f3]
        OFF = [LEN[0] * 2 + LEN[1], LEN[0] * 2, 0, LEN[0]]

        def part(buf, q):
            n = LEN[BRANCH[q][0]]
            return buf[:, OFF[q]:OFF[q] + n]

        def img(ap, n=HH):
            return ap.rearrange("p (h w) -> p h w", w=n)

        s_load = sem("s_load")
        s_stage = sem("s_stage")
        s_kron = sem("s_kron")
        s_set = sem("s_set")
        s_comb = sem("s_comb")
        s_zero = sem("s_zero")
        s_exp = sem("s_exp")
        stage = [d_a0[:, :, :].rearrange("p a b -> p (a b)")[:, 0:4 * KP], d_b0[:, :, :].rearrange("p a b -> p (a b)")[:, 0:4 * KP]]
        raw_dt = va[0:R_DT, :]
        raw_in = vb[:, 0:CH]
        raw_c1 = vc[:, 0:P]
        loads = [
            (ident[:, :], t["ident"]), (group_mean[:, :], t["group_mean"]), (chan_mean[:, :], t["chan_mean"]),
            (pick[:, :], t["pick"]), (ramp[:, :, :], t["ramp"]), (grid[:, :], t["grid"]),
            (conv_w[:, :, :, :], t["conv_w"]), (conv_b[:, :], t["conv_b"]), (neg_mw[:, :], t["mask_w"]),
            (filt[:, :], t["filt"]), (in_w[:, :, P:2 * P], t["in_z"]), (raw_in, t["in_x"]), (in_b[:, :], t["in_b"]), (raw_c1, t["c1_w"]),
            (c23_w[:, :, :, :], t["c23_w"]), (c_b[:, :], t["c_b"]), (out_w[:, :], t["out_w"]), (out_b[:, :], t["out_b"]),
            (bc_w[:, :, :, :], t["bc_w"]), (dt_b[:, :], t["dt_b"]), (a_neg[:, :, :], t["al"]), (dv[:, :], t["dv"]),
            (ln_g[:, :], t["ln_g"]), (ln_b[:, :], t["ln_b"]), (raw_dt[:, 0:6 * P], t["dt_parts"]),
            (up_k[0][KP:KP + 2, :, :], t["bias_on"][0]), (up_k[1][KP:KP + 2, :, :], t["bias_on"][1]),
            (xt[KP:KP + 2, :, :, :], t["bias_rows"]),
        ]
        with nc.Block() as block:
            @block.sync
            def _(sp):
                for dst, src in loads:
                    sp.dma_start(dst, src).then_inc(s_load, 16)
                for n in range(4):
                    if n:
                        sp.wait_ge(s_kron, 16 * n)
                    for a in range(2):
                        sp.dma_start(stage[a][0:KP, :], t["taps"][n, a]).then_inc(s_stage, 16)

            @block.vector
            def _(dve):
                for n in range(4):
                    dve.wait_ge(s_stage, 32 * (n + 1))
                    k = (up_k[n // 2] if n % 2 == 0 else
                         down_k[n // 2][:, :, :, :].rearrange("p k a b -> p k (a b)"))
                    for a in range(4):
                        for b in range(4):
                            nc.vector.scalar_tensor_tensor(
                                out=k[0:KP, 4 * a + b, :], in0=stage[0][0:KP, a * KP:(a + 1) * KP],
                                scalar=4.0 * UP_GAIN if n % 2 == 0 else 1.0,
                                in1=stage[1][0:KP, b * KP:(b + 1) * KP],
                                op0=ALU.mult, op1=ALU.mult).then_inc(s_kron, 1)
                dve.wait_ge(s_load, 16 * len(loads))
                nc.vector.tensor_copy(pick_bf[:, :], pick[:, :]).then_inc(s_set, 1)
                nc.vector.tensor_scalar(filt[:, :], filt[:, :], 1.0, -1.0, ALU.is_equal, ALU.mult).then_inc(s_set, 1)
                dve.wait_ge(s_set, 2)
                nc.vector.tensor_tensor(neg_mw[:, :], neg_mw[:, :], filt[:, :], ALU.mult).then_inc(s_set, 1)
                nc.vector.tensor_scalar(bias_sum[:, :], ln_b[:, 1:2], 3.0, ln_b[:, 0:1], ALU.mult, ALU.add).then_inc(s_set, 1)
                dve.wait_ge(s_set, 4)
                nc.vector.scalar_tensor_tensor(out=bias_sum[:, :], in0=ln_b[:, 2:3], scalar=2.0, in1=bias_sum[:, :],
                                               op0=ALU.mult, op1=ALU.add).then_inc(s_set, 1)
                dve.wait_ge(s_exp, 1)
                nc.vector.tensor_scalar(a_neg[:, :, :], a_neg[:, :, :], -1.0, None, ALU.mult).then_inc(s_set, 1)
                dve.wait_ge(s_comb, 3)
                nc.vector.tensor_copy(dt_w[:, :, :], ps[:, 0, 0:3 * P]).then_inc(s_set, 1)
                dve.wait_ge(s_comb, 6)
                nc.vector.tensor_copy(in_w[:, :, 0:P], ps[:, 1, 0:NC * P].rearrange("p (c m) -> p c m", c=NC)).then_inc(s_set, 1)
                nc.vector.tensor_tensor(c_b[:, 0:1], c_b[:, 0:1], ps[:, 1, NC * P:NC * P + 1], ALU.add).then_inc(s_set, 1)
                nc.vector.memset(eps[:, 0:1], GN_EPS).then_inc(s_set, 1)
                nc.vector.memset(eps[:, 1:2], LN_EPS).then_inc(s_set, 1)

            @block.gpsimd
            def _(pool):
                for buf in (pad[:, :, :, :], d_a1[:, :, :], d_b1[:, :, :], d_a2[:, :, :], d_b2[:, :, :]):
                    nc.gpsimd.memset(buf, 0.0).then_inc(s_zero, 1)

            @block.scalar
            def _(act):
                nc.scalar.preload_act_table_set("natural_log_exp_and_others")
                act.wait_ge(s_load, 16 * len(loads))
                nc.scalar.activation(a_neg[:, :, :], a_neg[:, :, :], ACT.Exp).then_inc(s_exp, 1)

            @block.tensor
            def _(pe):
                pe.wait_ge(s_load, 16 * len(loads))
                for w in range(3):
                    nc.tensor.matmul(ps[:, 0, w * P:(w + 1) * P], raw_dt[:, 2 * w * P:(2 * w + 1) * P],
                                     raw_dt[:, (2 * w + 1) * P:(2 * w + 2) * P], start=True, stop=True).then_inc(s_comb, 1)
                for c in range(NC):
                    nc.tensor.matmul(ps[:, 1, c * P:(c + 1) * P], raw_in[:, c * P:(c + 1) * P], raw_c1,
                                     start=True, stop=True).then_inc(s_comb, 1)
                nc.tensor.matmul(ps[:, 1, NC * P:NC * P + 1], raw_c1, in_b[:, 0:1], start=True, stop=True).then_inc(s_comb, 1)

        x_loaded = sem("x_loaded")
        y_stored = sem("y_stored")
        gn_vec = [sem("xgn_vec"), sem("bgn_vec")]
        gn_mm = [sem("xgn_mm"), sem("bgn_mm")]
        gn_act = [sem("xgn_act"), sem("bgn_act")]
        mask_vec = sem("mask_vec")
        mask_dist = sem("mask_dist")
        relu_done = sem("relu_done")
        conv_sum = sem("conv_sum")
        conv_added = sem("conv_added")
        turned = sem("turned")
        turn_copied = sem("turn_copied")
        up_sum = sem("up_sum")
        up_relu = sem("up_relu")
        up_leaky = sem("up_leaky")
        up_clipped = sem("up_clipped")
        down_sum = sem("down_sum")
        layer_added = sem("layer_added")
        x2_copied = sem("x2_copied")
        slot_full = sem("slot_full")
        f_copied = sem("f_copied")
        z_copied = sem("z_copied")
        gate_z = sem("gate_z")
        gate_exp = sem("gate_exp")
        gate_fin = sem("gate_fin")
        gate_mul = sem("gate_mul")
        v_act = sem("v_act")
        v_pool = sem("v_pool")
        v_series = sem("v_series")
        v_log = sem("v_log")
        delta_done = sem("delta_done")
        dx_done = sem("dx_done")
        hi_done = sem("hi_done")
        rest_done = sem("rest_done")
        mid_done = sem("mid_done")
        bct_done = sem("bct_done")
        da_done = sem("da_done")
        dbx_done = sem("dbx_done")
        scan_done = sem("scan_done")
        hc_done = sem("hc_done")
        state_added = sem("state_added")
        fold_done = sem("fold_done")
        y_done = sem("y_done")
        centred = sem("centred")
        squared = sem("squared")
        ln_rstd = sem("ln_rstd")
        y_normed = sem("y_normed")
        y_mixed = sem("y_mixed")
        gated = sem("gated")
        x3_done = sem("x3_done")
        turn_sems = SEMS[7:]

        POOL_COUNT = {j: i + 1 for i, j in enumerate(POOL_ADDS)}

        ADD_STEPS = {0: 1, 1: 3, 2: 3, 3: 2}

        def mixed_until(q):
            return sum(ADD_STEPS[i] for i in range(q))

        def da_view(k):
            q, g = SCAN_STEPS[k]
            return {0: d_a0[:, k % 2, :], 1: d_a1, 2: d_a2}[BRANCH[q][0]]

        def db_view(k):
            q, g = SCAN_STEPS[k]
            return {0: d_b0[:, k % 2, :], 1: d_b1, 2: d_b2}[BRANCH[q][0]]

        def h_view(j):
            lev = BRANCH[SCANS[j][1]][0]
            if lev == 0:
                return hs[:, j % NH, 0:HW]
            n = LEN[lev] + 1
            return hs[:, j % NH, 0:PER_STEP[lev] * n].rearrange("p (n l) -> p n l", l=n)

        def turn(block, has_b, has_last, has_first, load_at, store_at):
            USE = slot_uses([scan_layer_order()[k] for k in B_SEQUENCE])

            def slot(name):
                return ps[:, 4 + 2 * (USE[name] % 2):6 + 2 * (USE[name] % 2), :]

            def release(name):
                kind, i = name
                return {"b_in": (z_copied, 1), "b_f1": (f_copied, 1), "b_f2": (f_copied, 2), "b_f3": (f_copied, 3),
                        "V": (v_act, 4 * i + 1), "BC": (rest_done, i + 1), "B": (dbx_done, i + 1),
                        "C": (hc_done, LAST_SCAN.get(i, 0) + 1), "mean": (centred, i + 1),
                        "var": (ln_rstd, 2 * i + 1), "b_out": (x3_done, i + 1)}[kind]

            NAME_AT = {i: n for n, i in USE.items()}

            def full(name):
                return USE[name] + 1

            passes = (["last"] if has_last else []) + (["first"] if has_first else [])
            LAY = {"last": 1, "first": 0}
            order = turn_order(has_b, has_last, has_first)
            runs = [("conv", has_first), ("last", has_last), ("first", has_first)]
            inst = {which: n for n, which in enumerate(w for w, on in runs if on)}
            SRC = {"last": x3, "conv": xa, "first": xa}
            ACT_BASE, at = {}, 0
            for which in inst:
                ACT_BASE[which] = at
                at += 4 if which == "conv" else 10

            def normed(which, c):
                return ACT_BASE[which] + 2 + (c + 1) * (1 if which == "conv" else 4)

            def norm_width(q):
                lev = BRANCH[q][0]
                return LEN[lev] * (2 if lev else 1)

            def ring(p, c, k):
                return (2 * p + c) * (4 + N_UP) + k

            def bank(r):
                return ps[:, 2 + r % 2, :]

            def wait_bank(pe, r):
                if r >= 2:
                    pc, k = divmod(r - 2, 4 + N_UP)
                    if k < 4:
                        pe.wait_ge(turn_copied, 4 * pc + k + 1)
                    else:
                        pe.wait_ge(up_relu, 2 * (N_UP * pc + k - 4 + 1))

            def up_groups(u):
                at = 0
                for a, b in UP_STEPS[u]:
                    tiles = [(i, j) for i in TYPE_TILES[a] for j in TYPE_TILES[b]]
                    yield a, b, at, tiles
                    at += len(tiles) * P

            @block.sync
            def _(sp):
                if has_first:
                    sp.dma_start(xa[:, :, :], load_at).then_inc(x_loaded, 16)
                if has_last:
                    sp.wait_ge(layer_added, 4)
                    sp.dma_start(store_at, xg[:, :, :]).then_inc(y_stored, 16)
                    sp.wait_ge(y_stored, 16)

            @block.tensor
            def _(pe):
                def gn(x, i, n):
                    at = (ps[:, 0, 496:500] if x == 0 else ps[:, 4, 496:500])
                    if n == 1:
                        pe.wait_ge(gn_vec[x], 10 * i + 9)
                        nc.tensor.matmul(at[:, 2:4], group_mean[:, :], dev[x][:, 2, :], start=True, stop=True).then_inc(gn_mm[x], 1)
                    if n:
                        return
                    pe.wait_ge(gn_vec[x], 10 * i + 6)
                    if x == 0 and i:
                        if i == inst.get("first"):
                            if has_last:
                                pe.wait_ge(layer_added, 4)
                            pe.wait_ge(conv_added, 4)
                    nc.tensor.matmul(at[:, 0:2], group_mean[:, :], mv[x][:, :, 0], start=True, stop=True).then_inc(gn_mm[x], 1)

                def x_gn(which, n):
                    gn(0, inst[which], n)

                def conv(g, n):
                    m, half = divmod(g, 2)
                    if n == TAPS:
                        return
                    if g < 2 and n == 0:
                        pe.wait_ge(gn_vec[0], 10 * inst["conv"] + 10)
                        if has_last:
                            pe.wait_ge(layer_added, 4)
                    if g >= 2 and n == 0:
                        pe.wait_ge(conv_added, g - 1)
                    for i in range(2 * n, 2 * n + 2):
                        c, tap = divmod(i, TAPS)
                        if g < 2 and tap == 0:
                            pe.wait_ge(relu_done, c + 1)
                        r0 = half * (HH // 2) + tap // 3
                        mm = nc.tensor.matmul(ps[:, half, 0:HALF], conv_w[:, c, tap, m * P:(m + 1) * P],
                                              pad[:, c, r0:r0 + HH // 2, tap % 3:tap % 3 + WW],
                                              start=(i == 0), stop=(i == NC * TAPS - 1))
                    if n == TAPS - 1:
                        mm.then_inc(conv_sum, 1)

                def turn_patches(p, c, k):
                    pe.wait_ge(gn_act[0], normed(passes[p], c))
                    wait_bank(pe, ring(p, c, k))
                    out = bank(ring(p, c, k))
                    for j in range(4):
                        h0 = PATCH0[k]
                        mm = nc.tensor.transpose(out[0:KP, j * P:(j + 1) * P],
                                                 xp[:, c, j, h0 * TILE:(h0 + TILE) * TILE], ident[:, :])
                    mm.then_inc(turned, 1)

                def up(p, c, u):
                    pe.wait_ge(turn_copied, 4 * (2 * p + c) + 4)
                    wait_bank(pe, ring(p, c, 4 + u))
                    out = bank(ring(p, c, 4 + u))
                    for a, b, at, tiles in up_groups(u):
                        pa, pb = TYPE_PATCHES[a], TYPE_PATCHES[b]
                        x16 = xt[:, c, :, :].rearrange("p (i j) n -> p i j n", j=4)
                        mm = nc.tensor.matmul(out[0:KP, at:at + len(tiles) * P],
                                              up_k[LAY[passes[p]]][0:KP + 2, 4 * a + b, :],
                                              x16[0:KP + 2, pa[0]:pa[-1] + 1:2, pb[0]:pb[-1] + 1:2, :],
                                              start=True, stop=True)
                    mm.then_inc(up_sum, 1)

                def down(p, c, u):
                    y = N_UP * (2 * p + c) + u
                    pe.wait_ge(up_clipped, y + 1)
                    if u == 0:
                        if 2 * p + c:
                            pe.wait_ge(layer_added, 2 * (2 * p + c))
                        if passes[p] == "first":
                            pe.wait_ge(conv_added, 4)
                        pe.wait_ge(gn_vec[0], 10 * inst[passes[p]] + 10)
                    todo = []
                    for a, b, at, tiles in up_groups(u):
                        for n, (i, j) in enumerate(tiles):
                            r0, r1 = TILE_ROWS[i]
                            base = PATCH0[TILE_PATCH[i]]
                            for lo, hi, reg in ((r0, min(r1, SPLIT - base), 0), (max(r0, SPLIT - base), r1, 1)):
                                if lo < hi:
                                    todo.append((a, b, at + n * P, j, base, lo, hi, reg))
                    for a, b, col, j, base, lo, hi, reg in todo:
                        w0, w1 = TILE_ROWS[j]
                        wb = PATCH0[TILE_PATCH[j]]
                        rows = SPLIT if reg == 0 else HH - SPLIT
                        out = img(ps[:, reg, 0:rows * WW])[:, base + lo - reg * SPLIT:base + hi - reg * SPLIT, wb + w0:wb + w1]
                        mm = nc.tensor.matmul(out, ys[0:KP, y % NY, col:col + P],
                                              down_k[LAY[passes[p]]][0:KP, 4 * a + b, lo:hi, w0:w1],
                                              start=FRESH.pop((p, c, reg), True), stop=(u == N_UP - 1),
                                              skip_group_check=True)
                        FRESH[(p, c, reg)] = False
                    mm.then_inc(down_sum, 1)

                FRESH = {}

                def take(name):
                    i = USE[name]
                    if i >= 2:
                        pe.wait_ge(*release(NAME_AT[i - 2]))
                    return slot(name)

                def in_proj(name, m):
                    out = take(name)
                    for half in range(2):
                        for c in range(NC):
                            pe.wait_ge(gn_act[1], 3 + c)
                            mm = nc.tensor.matmul(out[:, half, 0:HALF], in_w[:, c, m * P:(m + 1) * P],
                                                  g2[:, c, half * HALF:(half + 1) * HALF], start=(c == 0), stop=(c == 1))
                    mm.then_inc(slot_full, 1)

                def b_gn(n):
                    gn(1, 0, n)

                def b_f1():
                    pe.wait_ge(gn_vec[1], 10)
                    in_proj(("b_f1", 0), 0)

                def b_in():
                    in_proj(("b_in", 0), 1)

                def shrink(name, src, side, lev, copied):
                    out = take(name)
                    pe.wait_ge(f_copied, copied)
                    v = img(src[:, :], side)
                    for tap in range(4):
                        mm = nc.tensor.matmul(out[:, 0, 0:LEN[lev]], c23_w[:, lev - 1, tap, :],
                                              v[:, tap // 2:side:2, tap % 2:side:2], start=(tap == 0), stop=(tap == 3))
                    mm.then_inc(slot_full, 1)

                def b_f2():
                    shrink(("b_f2", 0), f1, HH, 1, 1)

                def b_f3():
                    shrink(("b_f3", 0), f2, HH // 2, 2, 2)

                def halves(n):
                    return [(0, HALF), (1, HALF)] if n == HW else [(0, n)]

                def prep(q):
                    lev, w = BRANCH[q]
                    pe.wait_ge(f_copied, lev + 1)
                    for name, wt in (("V", dt_w[:, w, :]), ("BC", bc_w[:, w, :, :])):
                        out = take((name, q))
                        for half, n in halves(LEN[lev]):
                            mm = nc.tensor.matmul(out[:, half, 0:n], wt, F[lev][:, half * HALF:half * HALF + n], start=True, stop=True)
                        mm.then_inc(slot_full, 1)

                def cast(name, base, k):
                    q, g = SCAN_STEPS[k]
                    lev = BRANCH[q][0]
                    pe.wait_ge(bct_done, q + 1)
                    src = part(bct, q)
                    out = take((name, k))
                    if lev == 0:
                        for half in range(2):
                            mm = nc.tensor.matmul(out[:, half, 0:HALF],
                                                  pick_bf[:, base + g:base + g + 1].broadcast_to([P, P]),
                                                  src[:, half * HALF:(half + 1) * HALF], start=True, stop=True)
                    else:
                        n = LEN[lev]
                        per = PER_STEP[lev] // 2
                        for i in range(PER_STEP[lev]):
                            s = base + g * PER_STEP[lev] + i
                            mm = nc.tensor.matmul(out[:, i // per, (i % per) * n:(i % per + 1) * n],
                                                  pick_bf[:, s:s + 1].broadcast_to([P, P]), src, start=True, stop=True)
                    mm.then_inc(slot_full, 1)

                def cast_b(k):
                    cast("B", 0, k)

                def cast_c(k):
                    cast("C", N_STATE, k)

                def average(name, ready, q):
                    out = take((name, q))
                    pe.wait_ge(ready, q + 1)
                    for half, m in halves(norm_width(q)):
                        mm = nc.tensor.matmul(out[:, half, 0:m], chan_mean[:, :], va[:, half * HALF:half * HALF + m], start=True, stop=True)
                    mm.then_inc(slot_full, 1)

                def mean(q):
                    average("mean", y_done, q)

                def var(q):
                    average("var", squared, q)

                def b_out(m):
                    out = take(("b_out", m))
                    pe.wait_ge(gated, 1)
                    for half in range(2):
                        mm = nc.tensor.matmul(out[:, half, 0:HALF], out_w[:, m * P:(m + 1) * P],
                                              y1[:, half * HALF:(half + 1) * HALF], start=True, stop=True)
                    mm.then_inc(slot_full, 1)

                do = {"x_gn": x_gn, "conv": conv, "turn": turn_patches, "up": up, "down": down, "b_gn": b_gn, "b_in": b_in,
                      "b_f1": b_f1, "b_f2": b_f2, "b_f3": b_f3, "prep": prep, "cast_b": cast_b, "cast_c": cast_c, "mean": mean, "var": var, "b_out": b_out}
                for kind, *a in order:
                    if kind in do:
                        do[kind](*a)

            @block.scalar
            def _(act):
                def gn(x, i, n, base, src, free, parts):
                    at = (ps[:, 0, 496:500] if x == 0 else ps[:, 4, 496:500])
                    if n == 1:
                        act.wait_ge(gn_mm[x], 2 * i + 2)
                        nc.scalar.activation(lnv[x][:, :], at[:, 2:4], ACT.Ln, bias=eps[:, 0:1]).then_inc(gn_act[x], 1)
                        act.wait_ge(gn_act[x], base + 1)
                        nc.scalar.activation(rstd[x][:, :], lnv[x][:, :], ACT.Exp, scale=-0.5).then_inc(gn_act[x], 1)
                    if n < 2:
                        return
                    act.wait_ge(gn_vec[x], 10 * i + 10)
                    for s, v in free:
                        act.wait_ge(s, v)
                    c = n - 2
                    for dst, part_of in parts(c):
                        nc.scalar.activation(dst, part_of(src), ACT.Identity, bias=nbias[x][:, c:c + 1],
                                             scale=rstd[x][:, c:c + 1]).then_inc(gn_act[x], 1)

                def x_gn(which, n):
                    free = {"conv": [], "last": [(mask_vec, 21)] if has_first else [],
                            "first": [(y_stored, 16)] if has_last else [(mask_vec, 21)]}[which]

                    def parts(c):
                        if which == "conv":
                            return [(xg[:, c, :], lambda v: v[:, c, :])]
                        return [(img(xp[:, c, j, :], TILE), lambda v, j=j: img(v[:, c, :])[:, :, PATCH0[j]:PATCH0[j] + TILE])
                                for j in range(4)]

                    gn(0, inst[which], n, ACT_BASE[which], SRC[which], free, parts)

                def mask(n):
                    if n == 1:
                        act.wait_ge(mask_vec, 13)
                        for k in range(2):
                            for c in range(NC):
                                nc.scalar.activation(dist[:, k, c, :], grid[:, :], ACT.Abs,
                                                     bias=cen[:, 4, 2 * k + c:2 * k + c + 1]).then_inc(mask_dist, 1)
                    if n >= 3:
                        c = n - 3
                        act.wait_ge(mask_vec, 19 + 2 * c)
                        nc.scalar.activation(pad[:, c, 1:HH + 1, 1:WW + 1], img(msk[:, :]), ACT.Relu).then_inc(relu_done, 1)

                def turn_patches(p, c, k):
                    act.wait_ge(turned, 4 * (2 * p + c) + k + 1)
                    if p and k == 0:
                        act.wait_ge(up_sum, N_UP * (2 * p + c - 1))
                    nc.scalar.copy(xt[0:KP, c, 4 * k:4 * k + 4, :],
                                   bank(ring(p, c, k))[0:KP, :].rearrange("p (j n) -> p j n", n=P)).then_inc(turn_copied, 1)

                def up(p, c, u):
                    y = N_UP * (2 * p + c) + u
                    act.wait_ge(up_sum, y + 1)
                    if y >= NY:
                        act.wait_ge(down_sum, y - NY + 1)
                    z = bank(ring(p, c, 4 + u))[0:KP, :]
                    nc.scalar.activation(ys[0:KP, y % NY, :], z, ACT.Relu, scale=(1.0 - SLOPE) / SLOPE).then_inc(up_relu, 1)
                    if y:
                        act.wait_ge(up_leaky, y)
                    if has_first and y == 0:
                        act.wait_ge(relu_done, 2)
                    nc.scalar.copy(y_sloped[0:KP, :], z).then_inc(up_relu, 1)

                def b_gn(n):
                    gn(1, 0, n, 0, x2, [], lambda c: [(g2[:, c, :], lambda v: v[:, c, :])])

                def b_in():
                    act.wait_ge(slot_full, full(("b_in", 0)))
                    nc.scalar.activation(zs[:, :].rearrange("p (a b) -> p a b", a=2), slot(("b_in", 0))[:, :, 0:HALF],
                                         ACT.Identity, bias=in_b[:, 1:2]).then_inc(z_copied, 1)

                def gate_exponential():
                    act.wait_ge(gate_z, 1)
                    nc.scalar.activation(sz[:, :], sz[:, :], ACT.Exp, scale=-1.0).then_inc(gate_exp, 1)

                def b_f1():
                    act.wait_ge(slot_full, full(("b_f1", 0)))
                    nc.scalar.activation(f1[:, :].rearrange("p (a b) -> p a b", a=2), slot(("b_f1", 0))[:, :, 0:HALF],
                                         ACT.Identity, bias=c_b[:, 0:1]).then_inc(f_copied, 1)

                def b_f2():
                    act.wait_ge(slot_full, full(("b_f2", 0)))
                    nc.scalar.activation(f2[:, :], slot(("b_f2", 0))[:, 0, 0:LEN[1]], ACT.Identity, bias=c_b[:, 1:2]).then_inc(f_copied, 1)

                def b_f3():
                    act.wait_ge(slot_full, full(("b_f3", 0)))
                    nc.scalar.activation(f3[:, :], slot(("b_f3", 0))[:, 0, 0:LEN[2]], ACT.Identity, bias=c_b[:, 2:3]).then_inc(f_copied, 1)

                def wide(buf, n):
                    return buf[:, 0:n].rearrange("p (a b) -> p a b", a=2) if n == HW else buf[:, 0:n]

                def wide_ps(s, n, p0=0):
                    return s[p0:, :, 0:HALF] if n == HW else s[p0:, 0, 0:n]

                def prep(q):
                    lev, w = BRANCH[q]
                    n = LEN[lev]
                    act.wait_ge(slot_full, full(("V", q)))
                    if q:
                        act.wait_ge(delta_done, q)
                    nc.scalar.activation(wide(va, n), wide_ps(slot(("V", q)), n), ACT.Identity, bias=dt_b[:, w:w + 1]).then_inc(v_act, 1)
                    act.wait_ge(v_act, 4 * q + 1)
                    nc.scalar.activation(vb[:, 0:n], va[:, 0:n], ACT.Abs).then_inc(v_act, 1)
                    act.wait_ge(slot_full, full(("BC", q)))
                    nc.scalar.copy(wide(part(bct, q), n), wide_ps(slot(("BC", q)), n)).then_inc(hi_done, 1)
                    act.wait_ge(v_act, 4 * q + 2)
                    nc.scalar.activation(vb[:, 0:n], vb[:, 0:n], ACT.Exp, scale=-1.0).then_inc(v_act, 1)

                def split(q):
                    n = LEN[BRANCH[q][0]]
                    act.wait_ge(rest_done, q + 1)
                    nc.scalar.copy(part(bct, q)[64:, :], rest[64:, 0:n]).then_inc(mid_done, 1)
                    act.wait_ge(v_act, 4 * q + 3)
                    nc.scalar.activation(vc[:, 0:n], vb[:, 0:n], ACT.Ln, bias=1.0).then_inc(v_act, 1)

                def decay(k):
                    q, g = SCAN_STEPS[k]
                    lev, w = BRANCH[q]
                    act.wait_ge(delta_done, q + 1)
                    if k == 5:
                        act.wait_ge(slot_full, full(("b_in", 0)))
                    before = [j for j, s in enumerate(SCANS) if (s[0] == k - 2 and lev == 0 and k >= 7) or (s[0] == k - 1 and lev == 1 and g)]
                    if before:
                        act.wait_ge(scan_done, before[-1] + 1)
                    for i in range(PER_STEP[lev]):
                        s = g * PER_STEP[lev] + i
                        out = da_view(k) if lev == 0 else da_view(k)[:, i, 0:LEN[lev]]
                        nc.scalar.activation(out, part(delta, q), ACT.Exp, scale=a_neg[:, w, s:s + 1]).then_inc(da_done, 1)

                def centre(q):
                    n = norm_width(q)
                    act.wait_ge(centred, q + 1)
                    nc.scalar.activation(va[:, 0:n], vb[:, 0:n], ACT.Square).then_inc(squared, 1)

                def var(q):
                    n = norm_width(q)
                    act.wait_ge(slot_full, full(("var", q)))
                    nc.scalar.activation(wide(vc, n), wide_ps(slot(("var", q)), n), ACT.Ln, bias=eps[:, 1:2]).then_inc(ln_rstd, 1)
                    act.wait_ge(ln_rstd, 2 * q + 1)
                    nc.scalar.activation(vc[:, 0:n], vc[:, 0:n], ACT.Exp, scale=-0.5).then_inc(ln_rstd, 1)

                do = {"x_gn": x_gn, "mask": mask, "turn": turn_patches, "up": up, "b_gn": b_gn, "b_in": b_in, "gate_exp": gate_exponential,
                      "b_f1": b_f1, "b_f2": b_f2, "b_f3": b_f3, "prep": prep, "split": split, "decay": decay, "centre": centre, "var": var}
                for kind, *a in order:
                    if kind in do:
                        do[kind](*a)

            @block.gpsimd
            def _(pool):
                def keep():
                    if has_last:
                        pool.wait_ge(layer_added, 4)
                    nc.gpsimd.tensor_copy(x3[:, :, :], x2[:, :, :]).then_inc(x2_copied, 1)

                def gate_exp1():
                    pool.wait_ge(gate_exp, 1)
                    nc.gpsimd.tensor_scalar(sz[:, :], sz[:, :], 1.0, None, ALU.add).then_inc(gate_fin, 1)

                def leaky(p, c, u):
                    y = N_UP * (2 * p + c) + u
                    pool.wait_ge(up_relu, 2 * y + 2)
                    v = ys[0:KP, y % NY, :]
                    nc.gpsimd.tensor_tensor(v, y_sloped[0:KP, :], v, ALU.add).then_inc(up_leaky, 1)

                def gate_mul1():
                    pool.wait_ge(gate_mul, 1)
                    nc.gpsimd.tensor_tensor(sz[:, :], sz[:, :], zs[:, :], ALU.mult).then_inc(gate_fin, 1)

                def split(q):
                    n = LEN[BRANCH[q][0]]
                    pool.wait_ge(v_act, 4 * q + 3)
                    nc.gpsimd.tensor_scalar(poly[:, 0:n], vb[:, 0:n], 1.0 / 3.0, -0.5, ALU.mult, ALU.add).then_inc(v_pool, 1)
                    nc.gpsimd.tensor_scalar(far[:, 0:n], vb[:, 0:n], SERIES_UNTIL, None, ALU.is_ge).then_inc(v_pool, 1)
                    pool.wait_ge(v_pool, 3 * q + 1)
                    nc.gpsimd.tensor_tensor(poly[:, 0:n], poly[:, 0:n], vb[:, 0:n], ALU.mult).then_inc(v_pool, 1)

                def delta_x(q):
                    lev = BRANCH[q][0]
                    pool.wait_ge(delta_done, q + 1)
                    nc.gpsimd.tensor_tensor(part(dx, q), part(delta, q), F[lev][:, :], ALU.mult).then_inc(dx_done, 1)

                def add(k):
                    for j in SCANS_OF[k]:
                        if j not in POOL_COUNT:
                            continue
                        _, q, g, d = SCANS[j]
                        lev = BRANCH[q][0]
                        pool.wait_ge(hc_done, j + 1)
                        if POOL_COUNT[j] > 1:
                            pool.wait_ge(state_added, POOL_COUNT[j] - 1)
                        h = h_view(j) if lev == 0 else h_view(j)[:, :, 0:LEN[lev]]
                        a = acc[:, d, :] if lev == 0 else acc[:, d, :].rearrange("p (n l) -> p n l", l=LEN[lev])
                        nc.gpsimd.tensor_tensor(a, a, h, ALU.add).then_inc(state_added, 1)

                do = {"keep": keep, "up": leaky, "gate_exp": gate_exp1, "gate_mul": gate_mul1, "split": split, "delta": delta_x, "add": add}
                for kind, *a in order:
                    if kind in do:
                        do[kind](*a)

            @block.vector
            def _(dve):
                def gn(x, i, n, act_base, src):
                    b = 10 * i
                    at = (ps[:, 0, 496:500] if x == 0 else ps[:, 4, 496:500])
                    if n == 0:
                        for c in range(NC):
                            for half in range(2):
                                nc.vector.bn_stats(st[x][:, c, half, :], src[:, c, half * HALF:(half + 1) * HALF]).then_inc(gn_vec[x], 1)
                        dve.wait_ge(gn_vec[x], b + 4)
                        for c in range(NC):
                            nc.vector.bn_aggr(mv[x][:, c, :], st[x][:, c, :, :].rearrange("p a b -> p (a b)")).then_inc(gn_vec[x], 1)
                    if n == 1:
                        dve.wait_ge(gn_mm[x], 2 * i + 1)
                        dve.wait_ge(gn_vec[x], b + 6)
                        nc.vector.tensor_tensor(dev[x][:, 0, :], mv[x][:, :, 0], at[:, 0:2], ALU.subtract).then_inc(gn_vec[x], 1)
                        dve.wait_ge(gn_vec[x], b + 7)
                        nc.vector.tensor_tensor(dev[x][:, 1, :], dev[x][:, 0, :], dev[x][:, 0, :], ALU.mult).then_inc(gn_vec[x], 1)
                        dve.wait_ge(gn_vec[x], b + 8)
                        nc.vector.tensor_tensor(dev[x][:, 2, :], dev[x][:, 1, :], mv[x][:, :, 1], ALU.add).then_inc(gn_vec[x], 1)
                    if n == 2:
                        dve.wait_ge(gn_act[x], act_base + 2)
                        nc.vector.scalar_tensor_tensor(out=nbias[x][:, :], in0=at[:, 0:2], scalar=-1.0, in1=rstd[x][:, :],
                                                       op0=ALU.mult, op1=ALU.mult).then_inc(gn_vec[x], 1)

                def x_gn(which, n):
                    if which == "conv":
                        dve.wait_ge(x_loaded, 16)
                    if which == "first":
                        dve.wait_ge(conv_added, 4)
                    gn(0, inst[which], n, ACT_BASE[which], SRC[which])

                def b_gn(n):
                    gn(1, 0, n, 0, x2)

                def mask(part):
                    def step(ins):
                        ins.then_inc(mask_vec, 1)

                    if part == 0:
                        dve.wait_ge(gn_act[0], normed("conv", 1))
                        step(nc.vector.tensor_reduce(lines[:, 0, :, :], xg[:, :, :].rearrange("p c (h w) -> p c h w", w=WW), AX, ALU.add))
                        step(nc.vector.tensor_reduce(lines[:, 1, :, :], xg[:, :, :].rearrange("p c (h w) -> p c w h", w=WW), AX, ALU.add))
                    if part == 1:
                        dve.wait_ge(mask_vec, 2)
                        step(nc.vector.tensor_tensor(wlines[:, :, :, :].rearrange("p a c h -> p (a c) h"),
                                                     lines[:, :, :, :].rearrange("p a c h -> p (a c) h"), ramp[:, :, :], ALU.mult))
                        step(nc.vector.tensor_reduce(s0[:, :, :], lines[:, :, :, :], AX, ALU.add))
                        dve.wait_ge(mask_vec, 4)
                        step(nc.vector.tensor_reduce(s1[:, :, :], wlines[:, :, :, :], AX, ALU.add))
                        step(nc.vector.tensor_scalar(cen[:, 0, 0:2], s0[:, 0, :], 1e-9, None, ALU.max))
                        dve.wait_ge(mask_vec, 6)
                        step(nc.vector.reciprocal(cen[:, 0, 2:4], cen[:, 0, 0:2]))
                        dve.wait_ge(mask_vec, 7)
                        step(nc.vector.tensor_tensor(cen[:, 1, 0:2], s1[:, 0, :], cen[:, 0, 2:4], ALU.mult))
                        step(nc.vector.tensor_tensor(cen[:, 1, 2:4], s1[:, 1, :], cen[:, 0, 2:4], ALU.mult))
                        dve.wait_ge(mask_vec, 9)
                        step(nc.vector.tensor_scalar(cen[:, 2, :], cen[:, 1, :], 1.0, float(HH), ALU.max, ALU.min))
                        dve.wait_ge(mask_vec, 10)
                        step(nc.vector.tensor_scalar(cen[:, 3, :], cen[:, 2, :], MAGIC, None, ALU.add))
                        dve.wait_ge(mask_vec, 11)
                        step(nc.vector.tensor_scalar(cen[:, 2, :], cen[:, 3, :], MAGIC, None, ALU.subtract))
                        dve.wait_ge(mask_vec, 12)
                        step(nc.vector.tensor_scalar(cen[:, 4, :], cen[:, 2, :], 1.0, -STEP, ALU.subtract, ALU.mult))
                    if part == 2:
                        for k in range(2):
                            for c in range(NC):
                                dve.wait_ge(mask_dist, 2 * k + c + 1)
                                step(nc.vector.tensor_scalar(ahbw[:, k, c, :], dist[:, k, c, :], neg_mw[:, c:c + 1],
                                                             1.0 - k, ALU.mult, ALU.add))
                    if part >= 3:
                        c = part - 3
                        if c:
                            dve.wait_ge(relu_done, 1)
                        dve.wait_ge(mask_vec, 17 + 2 * c)
                        step(nc.vector.tensor_tensor(img(msk[:, :]), ahbw[:, 0, c, :].unsqueeze(2).broadcast_to([P, HH, WW]),
                                                     ahbw[:, 1, c, :].unsqueeze(1).broadcast_to([P, HH, WW]), ALU.add))
                        dve.wait_ge(mask_vec, 18 + 2 * c)
                        step(nc.vector.scalar_tensor_tensor(out=msk[:, :], in0=msk[:, :], scalar=-1.0, in1=xg[:, c, :],
                                                            op0=ALU.max, op1=ALU.mult))

                def conv(g, n):
                    if n < TAPS:
                        return
                    m, half = divmod(g, 2)
                    dve.wait_ge(conv_sum, g + 1)
                    v = xa[:, m, half * HALF:(half + 1) * HALF]
                    nc.vector.scalar_tensor_tensor(out=v, in0=ps[:, half, 0:HALF], scalar=conv_b[:, m:m + 1], in1=v,
                                                   op0=ALU.add, op1=ALU.add).then_inc(conv_added, 1)

                def clip(p, c, u):
                    y = N_UP * (2 * p + c) + u
                    v = ys[0:KP, y % NY, :]
                    dve.wait_ge(up_leaky, y + 1)
                    nc.vector.tensor_scalar(v, v, CLAMP, -CLAMP, ALU.min, ALU.max).then_inc(up_clipped, 1)

                def fin(p, c):
                    which = passes[p]
                    dve.wait_ge(down_sum, N_UP * (2 * p + c + 1))
                    src, dst = SRC[which], (xg if which == "last" else x2)
                    if which == "first" and has_b:
                        dve.wait_ge(gn_act[1], 4)
                        dve.wait_ge(x2_copied, 1)
                    for reg in range(2):
                        a, b = ((0, SPLIT * WW), (SPLIT * WW, HW))[reg]
                        nc.vector.tensor_tensor(dst[:, c, a:b], src[:, c, a:b], ps[:, reg, 0:b - a], ALU.add).then_inc(layer_added, 1)

                def gate_clamp():
                    dve.wait_ge(z_copied, 1)
                    nc.vector.tensor_scalar(sz[:, :], zs[:, :], -80.0, None, ALU.max).then_inc(gate_z, 1)

                def gate_reciprocal():
                    dve.wait_ge(gate_fin, 1)
                    nc.vector.reciprocal(sz[:, :], sz[:, :]).then_inc(gate_mul, 1)

                def split(q):
                    lev, w = BRANCH[q]
                    n = LEN[lev]
                    dve.wait_ge(hi_done, q + 1)
                    if q:
                        dve.wait_ge(bct_done, q)
                    s = slot(("BC", q))
                    if n == HW:
                        nc.vector.tensor_tensor(rest[64:, :].rearrange("p (a b) -> p a b", a=2), s[64:, :, 0:HALF],
                                                part(bct, q)[64:, :].rearrange("p (a b) -> p a b", a=2), ALU.subtract).then_inc(rest_done, 1)
                    else:
                        nc.vector.tensor_tensor(rest[64:, 0:n], s[64:, 0, 0:n], part(bct, q)[64:, :], ALU.subtract).then_inc(rest_done, 1)

                def delta_of(q):
                    n = LEN[BRANCH[q][0]]
                    dve.wait_ge(v_pool, 3 * q + 3)
                    nc.vector.scalar_tensor_tensor(out=poly[:, 0:n], in0=poly[:, 0:n], scalar=1.0, in1=vb[:, 0:n],
                                                   op0=ALU.add, op1=ALU.mult).then_inc(v_series, 1)
                    dve.wait_ge(v_series, q + 1)
                    dve.wait_ge(v_act, 4 * q + 4)
                    nc.vector.copy_predicated(poly[:, 0:n], far[:, 0:n].bitcast(mybir.dt.uint32), vc[:, 0:n]).then_inc(v_log, 1)
                    dve.wait_ge(v_log, q + 1)
                    nc.vector.scalar_tensor_tensor(out=part(delta, q), in0=va[:, 0:n], scalar=0.0, in1=poly[:, 0:n],
                                                   op0=ALU.max, op1=ALU.add).then_inc(delta_done, 1)
                    dve.wait_ge(mid_done, q + 1)
                    nc.vector.tensor_tensor(part(bct, q)[96:, :], rest[96:, 0:n], part(bct, q)[96:, :], ALU.subtract).then_inc(bct_done, 1)

                def dbx(k):
                    q, g = SCAN_STEPS[k]
                    lev, w = BRANCH[q]
                    dve.wait_ge(slot_full, full(("B", k)))
                    dve.wait_ge(dx_done, q + 1)
                    if k == 5:
                        dve.wait_ge(delta_done, 4)
                    s = slot(("B", k))[:, :, 0:HALF]
                    if lev == 0:
                        if k >= 7:
                            dve.wait_ge(scan_done, LAST_SCAN[k - 2] + 1)
                        nc.vector.tensor_tensor(db_view(k).rearrange("p (a b) -> p a b", a=2), s,
                                                part(dx, q).rearrange("p (a b) -> p a b", a=2), ALU.mult).then_inc(dbx_done, 1)
                    else:
                        n, per = LEN[lev], PER_STEP[lev] // 2
                        if lev == 1 and g:
                            dve.wait_ge(scan_done, LAST_SCAN[k - 1] + 1)
                        nc.vector.tensor_tensor(db_view(k)[:, :, 0:n].rearrange("p (a b) l -> p a b l", a=2),
                                                s.rearrange("p a (b l) -> p a b l", l=n),
                                                part(dx, q).unsqueeze(1).unsqueeze(1).broadcast_to([P, 2, per, n]),
                                                ALU.mult).then_inc(dbx_done, 1)

                def scan(k):
                    q, g = SCAN_STEPS[k]
                    lev = BRANCH[q][0]
                    done = sum(PER_STEP[BRANCH[SCAN_STEPS[i][0]][0]] for i in range(k + 1))
                    dve.wait_ge(da_done, done)
                    dve.wait_ge(dbx_done, k + 1)
                    for j in SCANS_OF[k]:
                        d = SCANS[j][3]
                        last = j - NH
                        if last in (0, 1):
                            dve.wait_ge(fold_done, 2)
                        elif last in POOL_COUNT:
                            dve.wait_ge(state_added, POOL_COUNT[last])
                        elif last >= 0:
                            dve.wait_ge(hc_done, last + 1)
                        n = HW if lev == 0 else PER_STEP[lev] * (LEN[lev] + 1)
                        a, b = [v if lev == 0 else v[:, :, :].rearrange("p n l -> p (n l)") for v in (da_view(k), db_view(k))]
                        h = hs[:, j % NH, 0:n]
                        if d:
                            a, b, h = a[:, ::-1], b[:, ::-1], h[:, ::-1]
                        nc.vector.tensor_tensor_scan(h, a, b, 0.0, ALU.mult, ALU.add).then_inc(scan_done, 1)

                def hc(k):
                    q, g = SCAN_STEPS[k]
                    lev = BRANCH[q][0]
                    dve.wait_ge(slot_full, full(("C", k)))
                    s = slot(("C", k))[:, :, 0:HALF]
                    for j in SCANS_OF[k]:
                        d = SCANS[j][3]
                        dve.wait_ge(scan_done, j + 1)
                        h = h_view(j)
                        if lev == 0:
                            h3 = h.rearrange("p (a b) -> p a b", a=2)
                            o = acc[:, d, :].rearrange("p (a b) -> p a b", a=2) if g == 0 else h3
                            if g == 0:
                                dve.wait_ge(fold_done, 4)
                        else:
                            n = LEN[lev]
                            h3 = h[:, :, 0:n].rearrange("p (a b) l -> p a b l", a=2)
                            s = slot(("C", k))[:, :, 0:HALF].rearrange("p a (b l) -> p a b l", l=n)
                            o = acc[:, d, :].rearrange("p (a b l) -> p a b l", a=2, l=n) if g == 0 and lev == 1 else h3
                        nc.vector.tensor_tensor(o, s, h3, ALU.mult).then_inc(hc_done, 1)

                def fold(q):
                    n = LEN[BRANCH[q][0]]
                    if q == 1:
                        dve.wait_ge(state_added, POOL_COUNT[max(j for j, s in enumerate(SCANS) if s[1] == 1)])
                        dve.wait_ge(bct_done, 4)
                    else:
                        dve.wait_ge(hc_done, 2)
                    for d in range(2):
                        src = (acc[:, d, :].rearrange("p (n l) -> p l n", l=n) if q == 1 else
                               h_view(d)[:, :, 0:n].rearrange("p n l -> p l n"))
                        nc.vector.tensor_reduce((sums3, rest)[q][:, d * n:(d + 1) * n], src, AX, ALU.add).then_inc(fold_done, 1)

                def y_of(q):
                    lev, w = BRANCH[q]
                    n = LEN[lev]
                    if q == 0:
                        dve.wait_ge(delta_done, 4)
                        dve.wait_ge(v_act, 16)
                    else:
                        dve.wait_ge(slot_full, full(("var", q - 1)))
                    if lev == 0:
                        dve.wait_ge(state_added, POOL_COUNT[max(j for j, s in enumerate(SCANS) if s[1] == q)])
                    else:
                        dve.wait_ge(fold_done, 2 * q + 2)
                    for d in range(2 if lev else 1):
                        src = acc[:, q - 2, :] if lev == 0 else (sums3, rest)[q][:, d * n:(d + 1) * n]
                        ins = nc.vector.scalar_tensor_tensor(out=va[:, d * n:(d + 1) * n], in0=F[lev][:, :], scalar=dv[:, w:w + 1],
                                                             in1=src, op0=ALU.mult, op1=ALU.add)
                    ins.then_inc(y_done, 1)

                def centre(q):
                    width = norm_width(q)
                    dve.wait_ge(slot_full, full(("mean", q)))
                    dve.wait_ge(y_done, q + 1)
                    if q:
                        dve.wait_ge(y_mixed, mixed_until(q))
                    s = slot(("mean", q))
                    if width == HW:
                        nc.vector.tensor_tensor(vb[:, :].rearrange("p (a b) -> p a b", a=2), va[:, :].rearrange("p (a b) -> p a b", a=2),
                                                s[:, :, 0:HALF], ALU.subtract).then_inc(centred, 1)
                    else:
                        nc.vector.tensor_tensor(vb[:, 0:width], va[:, 0:width], s[:, 0, 0:width], ALU.subtract).then_inc(centred, 1)

                def mix(q):
                    lev, w = BRANCH[q]
                    n, width = LEN[lev], norm_width(q)
                    dve.wait_ge(ln_rstd, 2 * q + 2)
                    dve.wait_ge(centred, q + 1)
                    g = ln_g[:, w:w + 1]
                    m = mixed_until(q)
                    if q == 3:
                        nc.vector.scalar_tensor_tensor(out=vb[:, :], in0=vb[:, :], scalar=g, in1=vc[:, :], op0=ALU.mult, op1=ALU.mult).then_inc(y_mixed, 1)
                        dve.wait_ge(y_mixed, m + 1)
                        nc.vector.tensor_tensor(y1[:, :], y1[:, :], vb[:, :], ALU.add).then_inc(y_mixed, 1)
                        return
                    if q == 2:
                        nc.vector.scalar_tensor_tensor(out=y1[:, :], in0=vb[:, :], scalar=g, in1=vc[:, :], op0=ALU.mult, op1=ALU.mult).then_inc(y_mixed, 1)
                        fine, coarse, side = y1, y2, HH
                    else:
                        nc.vector.scalar_tensor_tensor(out=vb[:, 0:width], in0=vb[:, 0:width], scalar=g, in1=vc[:, 0:width],
                                                       op0=ALU.mult, op1=ALU.mult).then_inc(y_normed, 1)
                        dve.wait_ge(y_normed, q + 1)
                        fine, coarse, side = (y3, None, 0) if q == 0 else (y2, y3, HH // 2)
                        nc.vector.tensor_tensor(fine[:, :], vb[:, 0:n], vb[:, n:2 * n], ALU.add).then_inc(y_mixed, 1)
                    if coarse is not None:
                        dve.wait_ge(y_mixed, m + 1)
                        for r in range(2):
                            o = img(fine[:, :], side)[:, r:side:2, :].rearrange("p h (w s) -> p h w s", s=2)
                            nc.vector.tensor_tensor(o, o, img(coarse[:, :], side // 2).unsqueeze(3).broadcast_to([P, side // 2, side // 2, 2]),
                                                    ALU.add).then_inc(y_mixed, 1)

                def gate():
                    dve.wait_ge(y_mixed, mixed_until(4))
                    dve.wait_ge(gate_fin, 2)
                    nc.vector.scalar_tensor_tensor(out=y1[:, :], in0=y1[:, :], scalar=bias_sum[:, 0:1], in1=sz[:, :],
                                                   op0=ALU.add, op1=ALU.mult).then_inc(gated, 1)

                def b_out(m):
                    dve.wait_ge(slot_full, full(("b_out", m)))
                    dve.wait_ge(x2_copied, 1)
                    v = x3[:, m, :].rearrange("p (a b) -> p a b", a=2)
                    nc.vector.scalar_tensor_tensor(out=v, in0=slot(("b_out", m))[:, :, 0:HALF], scalar=out_b[:, m:m + 1], in1=v,
                                                   op0=ALU.add, op1=ALU.add).then_inc(x3_done, 1)

                do = {"x_gn": x_gn, "mask": mask, "conv": conv, "clip": clip, "fin": fin, "b_gn": b_gn, "gate_z": gate_clamp, "gate_mul": gate_reciprocal, 
                      "split": split, "delta": delta_of, "dbx": dbx, "scan": scan, "hc": hc, "fold": fold, "y": y_of, "centre": centre,
                      "mix": mix, "gate": gate, "b_out": b_out}
                for kind, *a in order:
                    if kind in do:
                        do[kind](*a)

        def sample(arr, i):
            return arr[bass.ds(i, 1)].rearrange("o (c p) h w -> p (o c) (h w)", p=P)

        def between():
            ids = [s.num for s in turn_sems]
            nc.gpsimd.sem_clear(range(min(ids), max(ids) + 1))
            nc.all_engine_barrier()

        def run(i, has_b, has_last, has_first):
            with nc.Block() as block:
                turn(block, has_b, has_last, has_first,
                     sample(t["x"], i + 1) if has_first else None, sample(t["out"], i - 1) if has_last else None)
            between()

        run(-1, False, False, True)
        run(0, True, False, True)
        with nc.Fori(1, N_SAMPLES - 1) as i:
            run(i, True, True, True)
        run(N_SAMPLES - 1, True, True, False)
        run(N_SAMPLES, False, True, False)


def lay_out(inputs):
    import numpy as np
    g = {k: np.asarray(v) for k, v in inputs.items()}

    def cols(v):
        return np.ascontiguousarray(v.reshape(-1, P).T)

    L2 = {k[len("L2_conv_"):]: v for k, v in g.items() if k.startswith("L2_conv_")}
    a = {"x": g["x"]}
    a["conv_w"] = g["L0_conv_weight"].reshape(CH, NC, P, 9).transpose(2, 1, 3, 0)
    a["conv_b"] = cols(g["L0_conv_bias"])
    a["mask_w"] = cols(g["L0_conv_mask_weight"])
    a["filt"] = cols(g["L0_conv_filter"].reshape(-1))
    a["in_x"] = L2["in_w"][:P]
    a["in_z"] = L2["in_w"][P:].reshape(P, NC, P).transpose(2, 1, 0)
    a["in_b"] = cols(L2["in_b"])
    a["c1_w"] = L2["c1_w"].T
    a["c23_w"] = np.stack([L2["c2_w"], L2["c3_w"]]).reshape(2, P, P, 4).transpose(2, 0, 3, 1)
    a["c_b"] = np.stack([L2["c1_b"], L2["c2_b"], L2["c3_b"]], 1)
    a["out_w"] = L2["out_w"].T
    a["out_b"] = cols(L2["out_b"])
    xw = np.stack([L2[f"xw{i}"] for i in (1, 2, 3)])
    dtw = np.stack([L2[f"dtw{i}"] for i in (1, 2, 3)])
    bc = xw[:, R_DT:, :].transpose(2, 0, 1)
    a["bc_w"] = np.repeat(bc[:, :, None, :], 4, axis=2)
    a["dt_parts"] = np.stack([xw[:, :R_DT, :].transpose(1, 0, 2), dtw.transpose(2, 0, 1)], 2).reshape(R_DT, 6 * P)
    for name, key in (("dt_b", "dtb"), ("dv", "Dv"), ("ln_g", "g"), ("ln_b", "be")):
        a[name] = np.stack([L2[f"{key}{i}"] for i in (1, 2, 3)], 1)
    a["al"] = np.stack([L2[f"Al{i}"] for i in (1, 2, 3)], 1)
    taps = np.zeros((4, 2, KP, 4, KP), np.float32)
    i, j = np.divmod(np.arange(KP), TILE)
    for n in range(4):
        f = g[f"L{1 + 2 * (n // 2)}_conv_{'down' if n % 2 else 'up'}_filter"][::-1]
        line = np.concatenate([np.zeros(64, f.dtype), f, np.zeros(64, f.dtype)])
        for side, r in enumerate((i, j)):
            for k in range(4):
                if n % 2 == 0:
                    at = 2 * r[:, None] - r[None, :] + (11, 0, 1, -10)[k]
                else:
                    at = r[:, None] - 2 * r[None, :] + (0, 11, 10, 21)[k]
                taps[n, side, :, k, :] = line[at + 64]
    a["taps"] = taps.reshape(4, 2, KP, 4 * KP)
    b = np.stack([g["L1_conv_bias"], g["L3_conv_bias"]]).reshape(2, NC, 1, P)
    a["bias_rows"] = np.repeat(b, 16, axis=2)
    on = np.zeros((2, 2, 16, KP), np.float32)
    on[0, 0] = on[1, 1] = UP_GAIN
    a["bias_on"] = on
    n = np.arange(P)
    a["ident"] = np.eye(P, dtype=np.float32)
    a["group_mean"] = (n[:, None] // GROUP == n[None, :] // GROUP).astype(np.float32) / np.float32(GROUP)
    a["chan_mean"] = np.full((P, P), 1.0 / P, np.float32)
    pick = np.zeros((P, 2 * N_STATE), np.float32)
    for base in (0, 64, 96):
        pick[base:base + 32] = np.eye(32, dtype=np.float32)
    a["pick"] = pick
    a["ramp"] = np.tile(np.arange(1, HH + 1, dtype=np.float32), (P, 4, 1))
    a["grid"] = np.tile((np.arange(HH) * STEP).astype(np.float32), (P, 1))
    return {k: np.ascontiguousarray(v) for k, v in a.items()}


def kernel(**inputs):
    import concourse.bacc as _bacc
    from concourse.bass_utils import run_bass_kernel_spmd as _run

    nc = _bacc.Bacc("TRN2", target_bir_lowering=False, num_devices=1)
    arrays = lay_out(inputs)
    t = {k: nc.dram_tensor(f"in_{k}", v.shape, mybir.dt.from_np(v.dtype), kind="ExternalInput").ap() for k, v in arrays.items()}
    t["out"] = nc.dram_tensor("out_0", arrays["x"].shape, F32, kind="ExternalOutput").ap()
    build(nc, t)
    r = _run(nc, [{f"in_{k}": v for k, v in arrays.items()}], core_ids=[0])
    return r.results[0]["out_0"]
```
